# Optimizing a Trainium2 kernel written in Bass

```python
import numpy as np
import jax
import jax.numpy as jnp

def _softmax(x, axis=-1):
    return jax.nn.softmax(x, axis=axis)

def _gelu(x):
    return jax.nn.gelu(x, approximate=True)

def _silu(x):
    return jax.nn.silu(x)

def _sigmoid(x):
    return jax.nn.sigmoid(x)

def _layernorm(x, axis=-1, eps=1e-05):
    m = jnp.mean(x, axis=axis, keepdims=True)
    v = jnp.var(x, axis=axis, keepdims=True)
    return (x - m) / jnp.sqrt(v + eps)

def _scatter_add(tgt, idx, src, axis=0):
    return tgt.at[idx].add(src)

def _segment_sum(src, seg, n):
    return jax.ops.segment_sum(src, seg, n)
kernel_name = 'mk_gnn_resnorm_d4_gnn_r32_c13470'

def setup_inputs(seed: int=0):
    np.random.seed(seed)
    _w = jnp.asarray

    def _rec_inputs():
        import jax
        import jax.numpy as jnp
        _gk = jax.random.key(seed)
        x = -0.0003713 + 1 * jax.random.normal(jax.random.fold_in(_gk, 1), (3125, 128), jnp.float32)
        src = jax.random.randint(jax.random.fold_in(_gk, 2), (100000,), 0, 3125, jnp.int32)
        dst = jax.random.randint(jax.random.fold_in(_gk, 3), (100000,), 0, 3125, jnp.int32)
        _o = jnp.argsort(dst, stable=True)
        src = src[_o]
        dst = dst[_o]
        edge_type_8 = jax.random.randint(jax.random.fold_in(_gk, 13), (100000,), 0, 8, jnp.int32)
        return (x, src, dst, edge_type_8)
    x, src, dst, edge_type_8 = _rec_inputs()

    def _L0_gnn_setup():
        import jax, jax.numpy as jnp
        import numpy as np
        N = 3125
        E = 50000
        D = 128
        EPS = 1e-05

        def _layer_norm(h, g, b):
            mu = jnp.mean(h, axis=-1, keepdims=True)
            var = jnp.mean((h - mu) ** 2, axis=-1, keepdims=True)
            return (h - mu) * jax.lax.rsqrt(var + EPS) * g + b
        key = jax.random.key(seed)
        ks = jax.random.split(key, 6)
        x = jax.random.normal(ks[0], (N, D), dtype=jnp.float32)
        edge_row = jax.random.randint(ks[1], (E,), 0, N, dtype=jnp.int32)
        edge_col = jax.random.randint(ks[2], (E,), 0, N, dtype=jnp.int32)
        scale = 1.0 / np.sqrt(D)
        inp = {'x': x, 'edge_row': edge_row, 'edge_col': edge_col}
        for i, kk in zip((1, 2, 3), (ks[3], ks[4], ks[5])):
            inp[f'W{i}'] = jax.random.normal(kk, (D, D), dtype=jnp.float32) * scale
            inp[f'b{i}'] = jnp.zeros((D,), jnp.float32)
            inp[f'g{i}'] = jnp.ones((D,), jnp.float32)
            inp[f'beta{i}'] = jnp.zeros((D,), jnp.float32)
        return inp
    _L0_gnn_all = _L0_gnn_setup()
    _L0_gnn_in = {k: v for k, v in _L0_gnn_all.items() if k in ('W1', 'b1', 'g1', 'beta1', 'W2', 'b2', 'g2', 'beta2', 'W3', 'b3', 'g3', 'beta3')}
    del _L0_gnn_all

    def _L1_gnn_setup():
        import jax, jax.numpy as jnp
        import numpy as np
        N_NODES = 50000
        key = jax.random.key(seed)
        k1, k2, k3, k4 = jax.random.split(key, 4)
        x = jax.random.normal(k1, (N_NODES, 128), dtype=jnp.float32)
        edge_index = jax.random.randint(k2, (2, 25000), 0, N_NODES, dtype=jnp.int64)
        W = jax.random.normal(k3, (128, 128), dtype=jnp.float32) * (1.0 / np.sqrt(128))
        b = jax.random.normal(k4, (128,), dtype=jnp.float32) * 0.01
        return {'x': x, 'edge_index': edge_index, 'W': W, 'b': b}
    _L1_gnn_all = _L1_gnn_setup()
    _L1_gnn_in = {k: v for k, v in _L1_gnn_all.items() if k in ('W', 'b')}
    del _L1_gnn_all

    def _L2_gnn_setup():
        import jax, jax.numpy as jnp
        import numpy as np
        BN_EPS = 1e-05

        def _batchnorm(h, gamma, beta):
            mu = jnp.mean(h, axis=0)
            var = jnp.mean((h - mu) ** 2, axis=0)
            return (h - mu) * jax.lax.rsqrt(var + BN_EPS) * gamma + beta
        key = jax.random.key(seed)
        ks = jax.random.split(key, 8)
        N, E, D = (50000, 25000, 128)
        x = jax.random.normal(ks[0], (N, D), dtype=jnp.float32)
        edge_index = jax.random.randint(ks[1], (2, E), 0, N, dtype=jnp.int64)
        s1 = 1.0 / np.sqrt(D)
        W1 = jax.random.uniform(ks[2], (D, D), jnp.float32, -s1, s1)
        b1 = jax.random.uniform(ks[3], (D,), jnp.float32, -s1, s1)
        W2 = jax.random.uniform(ks[4], (D, D), jnp.float32, -s1, s1)
        b2 = jax.random.uniform(ks[5], (D,), jnp.float32, -s1, s1)
        g1 = jnp.ones((D,), jnp.float32)
        beta1 = jnp.zeros((D,), jnp.float32)
        g2 = jnp.ones((D,), jnp.float32)
        beta2 = jnp.zeros((D,), jnp.float32)
        eps = jnp.array([0.1], jnp.float32)
        return {'x': x, 'edge_index': edge_index, 'eps': eps, 'W1': W1, 'b1': b1, 'g1': g1, 'beta1': beta1, 'W2': W2, 'b2': b2, 'g2': g2, 'beta2': beta2}
    _L2_gnn_all = _L2_gnn_setup()
    _L2_gnn_in = {k: v for k, v in _L2_gnn_all.items() if k in ('eps', 'W1', 'b1', 'g1', 'beta1', 'W2', 'b2', 'g2', 'beta2')}
    del _L2_gnn_all

    def _L3_gnn_setup():
        import jax, jax.numpy as jnp
        import numpy as np
        NUM_RELS = 8

        def rgcn_layer(x, src, dst, etype, W, W_root, b, num_rels):
            N = x.shape[0]
            do = W.shape[-1]
            h = jnp.einsum('ni,rio->rno', x, W)
            msg = h[etype, src]
            seg = dst * num_rels + etype
            sums = jax.ops.segment_sum(msg, seg, num_segments=N * num_rels)
            cnt = jax.ops.segment_sum(jnp.ones(msg.shape[0], x.dtype), seg, num_segments=N * num_rels)
            mean = sums / jnp.maximum(cnt, 1.0)[:, None]
            agg = mean.reshape(N, num_rels, do).sum(axis=1)
            return agg + x @ W_root + b
        key = jax.random.key(seed)
        ks = jax.random.split(key, 10)
        N, E = (50000, 18750)
        di, dh, do, R = (128, 256, 128, NUM_RELS)
        x = jax.random.normal(ks[0], (N, di), dtype=jnp.float32)
        edge_index = jax.random.randint(ks[1], (2, E), 0, N, dtype=jnp.int64)
        edge_type = jax.random.randint(ks[2], (E,), 0, R, dtype=jnp.int64)
        s1 = 1.0 / np.sqrt(di)
        s2 = 1.0 / np.sqrt(dh)
        W1 = jax.random.normal(ks[3], (R, di, dh), dtype=jnp.float32) * s1
        root1 = jax.random.normal(ks[4], (di, dh), dtype=jnp.float32) * s1
        b1 = jnp.zeros((dh,), jnp.float32)
        W2 = jax.random.normal(ks[5], (R, dh, do), dtype=jnp.float32) * s2
        root2 = jax.random.normal(ks[6], (dh, do), dtype=jnp.float32) * s2
        b2 = jnp.zeros((do,), jnp.float32)
        return {'x': x, 'edge_index': edge_index, 'edge_type': edge_type, 'W1': W1, 'root1': root1, 'b1': b1, 'W2': W2, 'root2': root2, 'b2': b2}
    _L3_gnn_all = _L3_gnn_setup()
    _L3_gnn_in = {k: v for k, v in _L3_gnn_all.items() if k in ('W1', 'root1', 'b1', 'W2', 'root2', 'b2')}
    del _L3_gnn_all
    return {'x': x, 'src': src, 'dst': dst, 'edge_type_8': edge_type_8, 'L0_gnn_W1': _L0_gnn_in['W1'], 'L0_gnn_b1': _L0_gnn_in['b1'], 'L0_gnn_g1': _L0_gnn_in['g1'], 'L0_gnn_beta1': _L0_gnn_in['beta1'], 'L0_gnn_W2': _L0_gnn_in['W2'], 'L0_gnn_b2': _L0_gnn_in['b2'], 'L0_gnn_g2': _L0_gnn_in['g2'], 'L0_gnn_beta2': _L0_gnn_in['beta2'], 'L0_gnn_W3': _L0_gnn_in['W3'], 'L0_gnn_b3': _L0_gnn_in['b3'], 'L0_gnn_g3': _L0_gnn_in['g3'], 'L0_gnn_beta3': _L0_gnn_in['beta3'], 'L1_gnn_W': _L1_gnn_in['W'], 'L1_gnn_b': _L1_gnn_in['b'], 'L2_gnn_eps': _L2_gnn_in['eps'], 'L2_gnn_W1': _L2_gnn_in['W1'], 'L2_gnn_b1': _L2_gnn_in['b1'], 'L2_gnn_g1': _L2_gnn_in['g1'], 'L2_gnn_beta1': _L2_gnn_in['beta1'], 'L2_gnn_W2': _L2_gnn_in['W2'], 'L2_gnn_b2': _L2_gnn_in['b2'], 'L2_gnn_g2': _L2_gnn_in['g2'], 'L2_gnn_beta2': _L2_gnn_in['beta2'], 'L3_gnn_W1': _L3_gnn_in['W1'], 'L3_gnn_root1': _L3_gnn_in['root1'], 'L3_gnn_b1': _L3_gnn_in['b1'], 'L3_gnn_W2': _L3_gnn_in['W2'], 'L3_gnn_root2': _L3_gnn_in['root2'], 'L3_gnn_b2': _L3_gnn_in['b2']}

def reference(x, src, dst, edge_type_8, L0_gnn_W1, L0_gnn_b1, L0_gnn_g1, L0_gnn_beta1, L0_gnn_W2, L0_gnn_b2, L0_gnn_g2, L0_gnn_beta2, L0_gnn_W3, L0_gnn_b3, L0_gnn_g3, L0_gnn_beta3, L1_gnn_W, L1_gnn_b, L2_gnn_eps, L2_gnn_W1, L2_gnn_b1, L2_gnn_g1, L2_gnn_beta1, L2_gnn_W2, L2_gnn_b2, L2_gnn_g2, L2_gnn_beta2, L3_gnn_W1, L3_gnn_root1, L3_gnn_b1, L3_gnn_W2, L3_gnn_root2, L3_gnn_b2):
    import jax
    import jax.numpy as jnp

    def _L0_gnn_ref(x, W1, b1, g1, beta1, W2, b2, g2, beta2, W3, b3, g3, beta3, edge_row, edge_col):
        import jax, jax.numpy as jnp
        import numpy as np
        N = 3125
        E = 50000
        D = 128
        EPS = 1e-05

        def _layer_norm(h, g, b):
            mu = jnp.mean(h, axis=-1, keepdims=True)
            var = jnp.mean((h - mu) ** 2, axis=-1, keepdims=True)
            return (h - mu) * jax.lax.rsqrt(var + EPS) * g + b
        n = x.shape[0]
        loops = jnp.arange(n, dtype=edge_row.dtype)
        row = jnp.concatenate([edge_row, loops])
        col = jnp.concatenate([edge_col, loops])
        deg = jax.ops.segment_sum(jnp.ones(row.shape[0], dtype=x.dtype), row, num_segments=n)
        dinv = jnp.where(deg > 0, jax.lax.rsqrt(deg), 0.0)
        w = dinv[row] * dinv[col]

        def gcn_layer(h, W, b, g, beta):
            h = h @ W
            msg = w[:, None] * h[col]
            h = jax.ops.segment_sum(msg, row, num_segments=n) + b
            return jax.nn.relu(_layer_norm(h, g, beta))
        h = gcn_layer(x, W1, b1, g1, beta1)
        h = gcn_layer(h, W2, b2, g2, beta2)
        h = gcn_layer(h, W3, b3, g3, beta3)
        return h

    def _L1_gnn_ref(x, edge_index, W, b):
        import jax, jax.numpy as jnp
        import numpy as np
        N_NODES = 50000
        n = x.shape[0]
        loops = jnp.arange(n, dtype=edge_index.dtype)
        src = jnp.concatenate([edge_index[0], loops])
        dst = jnp.concatenate([edge_index[1], loops])
        h = x @ W.T + b
        msgs = h[src]
        out = jax.ops.segment_sum(msgs, dst, num_segments=n)
        return out

    def _L2_gnn_ref(x, edge_index, eps, W1, b1, g1, beta1, W2, b2, g2, beta2):
        import jax, jax.numpy as jnp
        import numpy as np
        BN_EPS = 1e-05

        def _batchnorm(h, gamma, beta):
            mu = jnp.mean(h, axis=0)
            var = jnp.mean((h - mu) ** 2, axis=0)
            return (h - mu) * jax.lax.rsqrt(var + BN_EPS) * gamma + beta
        src, dst = (edge_index[0], edge_index[1])
        N = x.shape[0]
        aggr = jax.ops.segment_sum(x[src], dst, num_segments=N)
        out = (1.0 + eps) * x + aggr
        h = jax.nn.relu(_batchnorm(out @ W1 + b1, g1, beta1))
        h = jax.nn.relu(_batchnorm(h @ W2 + b2, g2, beta2))
        return h

    def _L3_gnn_ref(x, edge_index, edge_type, W1, root1, b1, W2, root2, b2):
        import jax, jax.numpy as jnp
        import numpy as np
        NUM_RELS = 8

        def rgcn_layer(x, src, dst, etype, W, W_root, b, num_rels):
            N = x.shape[0]
            do = W.shape[-1]
            h = jnp.einsum('ni,rio->rno', x, W)
            msg = h[etype, src]
            seg = dst * num_rels + etype
            sums = jax.ops.segment_sum(msg, seg, num_segments=N * num_rels)
            cnt = jax.ops.segment_sum(jnp.ones(msg.shape[0], x.dtype), seg, num_segments=N * num_rels)
            mean = sums / jnp.maximum(cnt, 1.0)[:, None]
            agg = mean.reshape(N, num_rels, do).sum(axis=1)
            return agg + x @ W_root + b
        src, dst = (edge_index[0], edge_index[1])
        h = rgcn_layer(x, src, dst, edge_type, W1, root1, b1, NUM_RELS)
        h = jax.nn.relu(h)
        return rgcn_layer(h, src, dst, edge_type, W2, root2, b2, NUM_RELS)
    edge_index = jnp.stack([src, dst])
    x = _layernorm(x + _L0_gnn_ref(x, L0_gnn_W1, L0_gnn_b1, L0_gnn_g1, L0_gnn_beta1, L0_gnn_W2, L0_gnn_b2, L0_gnn_g2, L0_gnn_beta2, L0_gnn_W3, L0_gnn_b3, L0_gnn_g3, L0_gnn_beta3, src, dst), axis=-1)
    x = _layernorm(x + _L1_gnn_ref(x, edge_index, L1_gnn_W, L1_gnn_b), axis=-1)
    x = _layernorm(x + _L2_gnn_ref(x, edge_index, L2_gnn_eps, L2_gnn_W1, L2_gnn_b1, L2_gnn_g1, L2_gnn_beta1, L2_gnn_W2, L2_gnn_b2, L2_gnn_g2, L2_gnn_beta2), axis=-1)
    x = _layernorm(x + _L3_gnn_ref(x, edge_index, edge_type_8, L3_gnn_W1, L3_gnn_root1, L3_gnn_b1, L3_gnn_W2, L3_gnn_root2, L3_gnn_b2), axis=-1)
    return x

_drawn_inputs = setup_inputs


def setup_inputs(seed=0):
    import zlib

    import numpy as np

    out = dict(_drawn_inputs(seed))
    spreads = {'L0_gnn_b1': (0.0, 0.1),
     'L0_gnn_g1': (1.0, 0.2),
     'L0_gnn_beta1': (0.0, 0.1),
     'L0_gnn_b2': (0.0, 0.1),
     'L0_gnn_g2': (1.0, 0.2),
     'L0_gnn_beta2': (0.0, 0.1),
     'L0_gnn_b3': (0.0, 0.1),
     'L0_gnn_g3': (1.0, 0.2),
     'L0_gnn_beta3': (0.0, 0.1),
     'L2_gnn_g1': (1.0, 0.2),
     'L2_gnn_beta1': (0.0, 0.1),
     'L2_gnn_g2': (1.0, 0.2),
     'L2_gnn_beta2': (0.0, 0.1),
     'L3_gnn_b1': (0.0, 0.1),
     'L3_gnn_b2': (0.0, 0.515)}
    factors = {'L1_gnn_b': 3.083, 'L2_gnn_b1': 8.0, 'L2_gnn_b2': 8.0}
    for name, (base, spread) in spreads.items():
        noise = np.random.default_rng([zlib.crc32(name.encode()), seed]).standard_normal(out[name].shape)
        drawn = base * np.exp(spread * noise) if base else spread * noise
        out[name] = jnp.asarray(drawn.astype(out[name].dtype))
    for name, factor in factors.items():
        out[name] = (out[name] * factor).astype(out[name].dtype)
    return out
```

```python
from contextlib import ExitStack

import concourse.bass as bass
from concourse import mybir

ALU = mybir.AluOpType
ACT = mybir.ActivationFunctionType
AX = mybir.AxisListType
F32 = mybir.dt.float32
F16 = mybir.dt.float16
BF16 = mybir.dt.bfloat16
I32 = mybir.dt.int32
U32 = mybir.dt.uint32

P = 128
EPS = 1e-5
REL = 8
ROW_LOG2 = 7
WA = 8
WA_LOG2 = 3
WR = 32
WR_LOG2 = 5
REGS = 32
AHEAD = 3


class Lane:

    def __init__(self, sem):
        self.sem, self.count, self.program, self.seen = sem, 0, [], {}

    def wait(self, *tokens):
        for token in tokens:
            if token is None:
                continue
            sem, value = token
            if self.seen.get(id(sem), 0) < value:
                self.seen[id(sem)] = value
                self.program.append(lambda e, s=sem, v=value: e.wait_ge(s, v))

    def do(self, emit, *tokens):
        self.wait(*tokens)
        self.count += 1
        self.program.append(lambda e, f=emit, s=self.sem: f(e).then_inc(s, 1))
        return (self.sem, self.count)

    def quiet(self, emit, *tokens):
        self.wait(*tokens)
        self.program.append(lambda e, f=emit: f(e))

    def dma(self, out, in_, channel, *tokens, **how):
        self.wait(*tokens)
        channel[1] += 16
        self.program.append(lambda e, s=channel[0]: e.dma_start(out, in_, **how).then_inc(s, 16))
        return (channel[0], channel[1])

    def last(self):
        return (self.sem, self.count) if self.count else None

    def replay(self, e):
        for step in self.program:
            step(e)


def gnn_stack(nc, io, out):
    N, D = io["x"].shape
    E = io["src"].shape[0]
    NB = -(-N // P)
    NP = NB * P
    FULL = N // P
    TAILN = N - FULL * P
    T = -(-E // P)
    TB = -(-T // P)
    TFULL = (E // P) // P
    TROWS = E // P - TFULL * P
    TREST = E - (E // P) * P
    TLAST = T - TFULL * P
    JA = T + -(-N // WA) - 1
    JR = T + -(-N // WR) - 1
    H = io["L3_gnn_W1"].shape[2]
    HB = H // P
    CH = 512
    NCH = -(-NP // CH)
    chunk = [(c * CH, min(CH, NP - c * CH)) for c in range(NCH)]
    G = WR * REL // P
    GN = P // REL
    NW4 = NB * P // WR
    WPB = P // WR
    FX = 1024.0

    ctx = ExitStack()
    with ctx:
        def sem(name):
            return ctx.enter_context(nc.semaphore(name))

        def channel(name):
            return [sem(name), 0]

        def sb(name, shape, dt, where=None):
            return (where or ctx).enter_context(nc.sbuf_tensor(name, shape, dt))

        pe, dve, act, pool, sp = (Lane(sem(f"s_{n}")) for n in ("pe", "dve", "act", "pool", "sp"))
        bank = [ctx.enter_context(nc.psum_tensor(f"bank{i}", [P, CH], F32)) for i in range(8)]

        ident = sb("ident", [P, P], F32)
        ident16 = sb("ident16", [P, P], F16)
        ones16 = sb("ones16", [P, 1], F16)
        ones_row = sb("ones_row", [1, P], F32)
        xres = sb("xres", [P, NB, D], F32)
        zT = sb("zT", [P, NP], F32)
        znode = zT[:, :].rearrange("p (b d) -> p b d", d=D)
        stats = sb("stats", [P, NB, 6], F32)
        mv = sb("mv", [P, NB, 2], F32)
        rstd = sb("rstd", [P, NB], F32)
        root = sb("root", [P, 2, NB], F32)
        nmr = sb("nmr", [P, NB], F32)
        small = sb("small", [P, 16], F32)
        smalli = sb("smalli", [P, 2], I32)
        rows = sb("rows", [P, 12, D], F32)
        colp = sb("colp", [P, 16], F32)

        scr_w = nc.dram_tensor("scr_windows", [1, JR], I32, kind="Internal").ap()
        scr_i = nc.dram_tensor("scr_index", [P, 2, JR], I32, kind="Internal").ap()
        scr_c = nc.dram_tensor("scr_code", [P, JR], F32, kind="Internal").ap()
        table1 = nc.dram_tensor("table1", [NP, 3 * D], BF16, kind="Internal").ap()
        table2 = nc.dram_tensor("table2", [NP * REL, 3 * D], BF16, kind="Internal").ap()

        m0 = pool.do(lambda e: e.memset(ident[:, :], 0.0))
        m1 = pool.do(lambda e: e.affine_select(out=ident[:, :], in_=ident[:, :], compare_op=ALU.not_equal,
                                               fill=1.0, base=0, pattern=[[-1, P]], channel_multiplier=1), m0)
        t_ident = pool.do(lambda e: e.tensor_copy(ident16[:, :], ident[:, :]), m1)
        pool.do(lambda e: e.memset(ones_row[:, :], 1.0))
        t_const = pool.do(lambda e: e.memset(ones16[:, :], 1.0))

        ch_x, ch_p = channel("ch_x"), channel("ch_param")
        m2 = dve.do(lambda e: e.memset(xres[:, FULL, :], 0.0))
        sp.dma(xres[:, 0:FULL, :], io["x"][0:FULL * P, :].rearrange("(b p) d -> p b d", p=P), ch_x)
        t_x = sp.dma(xres[0:TAILN, FULL, :], io["x"][FULL * P:N, :], ch_x, m2)

        ROW = {}
        for k, name in enumerate(["L0_gnn_b1", "L0_gnn_g1", "L0_gnn_beta1", "L0_gnn_b2", "L0_gnn_g2",
                                  "L0_gnn_beta2", "L0_gnn_b3", "L0_gnn_g3", "L0_gnn_beta3", "L1_gnn_b",
                                  "L3_gnn_b2"]):
            ROW[name] = rows[:, k, :]
            act.dma(rows[:, k, :], io[name].rearrange("(a d) -> a d", a=1).broadcast_to([P, D]), ch_p)
        COL = {}
        for k, name in enumerate(["L2_gnn_b1", "L2_gnn_g1", "L2_gnn_beta1", "L2_gnn_b2", "L2_gnn_g2",
                                  "L2_gnn_beta2"]):
            COL[name] = colp[:, k:k + 1]
            act.dma(colp[:, k:k + 1], io[name].rearrange("(d a) -> d a", a=1), ch_p)
        for h in range(HB):
            act.dma(colp[:, 8 + h:9 + h], io["L3_gnn_b1"][h * P:h * P + P].rearrange("(d a) -> d a", a=1), ch_p)
        t_param = act.dma(colp[:, 10:11], io["L2_gnn_eps"].rearrange("(a d) -> a d", a=1).broadcast_to([P, 1]), ch_p)

        adj_ctx = ExitStack()
        adj = sb("adj", [P, NB, NP], F16, adj_ctx)
        own = ExitStack()
        flat = adj[:, :, :].rearrange("p b n -> p (b n)").bitcast(F32)
        carved = [0]

        def carve(shape, dt=F32):
            n = 1
            for k in shape[1:]:
                n *= k
            v = flat[0:shape[0], carved[0]:carved[0] + n]
            carved[0] += n
            if dt != F32:
                v = v.bitcast(dt)
            if len(shape) == 3:
                v = v.rearrange("p (a b) -> p a b", b=shape[2])
            if len(shape) == 4:
                v = v.rearrange("p (a b c) -> p a b c", b=shape[2], c=shape[3])
            return v
        slo = zT[:, 0:JA]
        code = zT[:, JA:2 * JA]
        wcol = sb("wcol", [1, JA], I32, own)
        tab_i = carve([P, 3, TB, P], I32)
        tab = carve([P, 3, TB, P], F32)
        prev_i = carve([P, TB], I32)
        steps = carve([P, JA], F32)
        ends = carve([P, 4, TB], F32)
        tcol = carve([P, TB], F32)
        tmp_i = carve([P, TB], I32)
        pick = carve([P, 2, 2, CH], F32)
        exp_i = carve([P, 3, CH], I32)
        exp_f = carve([P, 4, CH], F32)
        out_i = carve([P, 2, CH], I32)
        out_c = carve([P, CH], F32)
        wrow = carve([1, CH], F32)
        wrow_i = carve([1, CH], I32)
        tabw = carve([P, 2, TB, P], F32)

        free_end = NB * NP // 2
        t_zero_rest = pool.do(lambda e: e.memset(flat[:, carved[0]:free_end], 0.0))

        q0 = dve.do(lambda e: e.memset(tab_i[:, :, TFULL, :], 0))
        q1 = dve.do(lambda e: e.memset(tab_i[:, 1, TFULL, :], NP + 4095), q0)
        q2 = dve.do(lambda e: e.memset(prev_i[:, :], 0))
        ch_t = [channel(f"ch_tab{i}") for i in range(3)]
        t_tab = []
        for i, name in enumerate(["src", "dst", "edge_type_8"]):
            e1 = io[name]
            n0 = TFULL * P * P
            sp.dma(tab_i[:, i, 0:TFULL, :], e1[0:n0].rearrange("(b q e) -> q b e", q=P, e=P), ch_t[i])
            sp.dma(tab_i[0:TROWS, i, TFULL, :], e1[n0:n0 + TROWS * P].rearrange("(q e) -> q e", e=P), ch_t[i], q1)
            t_tab.append(sp.dma(tab_i[TROWS:TROWS + 1, i, TFULL, 0:TREST],
                                e1[n0 + TROWS * P:E].rearrange("(q e) -> q e", q=1), ch_t[i]))
        ch_v = channel("ch_prev")
        dst2 = io["dst"][0:(E // P) * P].rearrange("(t e) -> t e", e=P)[:, P - 1:P]
        act.dma(prev_i[1:P, 0:1], dst2[0:P - 1, :], ch_v, q2, allow_slow_non_contiguous=True)
        for b in range(1, TB):
            n = min(P, T - b * P)
            t_prev = act.dma(prev_i[0:n, b:b + 1], dst2[b * P - 1:b * P - 1 + n, :], ch_v,
                             allow_slow_non_contiguous=True)

        i0 = pool.do(lambda e: e.iota(steps[:, :], pattern=[[1, JA]], base=0, channel_multiplier=0,
                                      allow_small_or_imprecise_dtypes=True))
        i1 = pool.do(lambda e: e.iota(tcol[:, :], pattern=[[P, TB]], base=0, channel_multiplier=1,
                                      allow_small_or_imprecise_dtypes=True))
        c0 = dve.do(lambda e: e.tensor_copy(tab[:, :, :, :], tab_i[:, :, :, :]), *t_tab)
        ends_tok = {}
        for k, lg in ((0, WA_LOG2), (1, WR_LOG2)):
            a = dve.do(lambda e, lg=lg: e.tensor_scalar(tmp_i[:, :], tab_i[:, 1, :, P - 1], lg, None,
                                                        ALU.logical_shift_right), c0, dve.last())
            a = dve.do(lambda e, k=k: e.tensor_tensor(ends[:, 2 * k, :], tmp_i[:, :], tcol[:, :], ALU.add), a, i1)
            a = dve.do(lambda e, lg=lg: e.tensor_scalar(tmp_i[:, :], prev_i[:, :], lg, None,
                                                        ALU.logical_shift_right), a, t_prev)
            a = dve.do(lambda e, k=k: e.scalar_tensor_tensor(out=ends[:, 2 * k + 1, :], in0=tmp_i[:, :], scalar=-1.0,
                                                             in1=tcol[:, :], op0=ALU.add, op1=ALU.add), a)
            a = dve.do(lambda e, k=k, W=(WA, WR)[k]: e.scalar_tensor_tensor(
                out=tabw[:, k, :, :], in0=tcol[:, :].unsqueeze(2).broadcast_to([P, TB, P]), scalar=float(W),
                in1=tab[:, 1, :, :], op0=ALU.mult, op1=ALU.add), a)
            ends_tok[k] = a
        t_ends = dve.do(lambda e: e.memset(ends[0:1, 1:4:2, 0:1], -1.0), dve.last())

        plan_done = []
        ch_s = channel("ch_plan")
        pick_free = [None, None]
        psum_free = None
        store_free = None
        npick = 0
        for k, J in ((1, JR), (0, JA)):
            for a0 in range(0, J, CH):
                n = min(CH, J - a0)
                for b in range(TB):
                    rws = P if b < TFULL else TLAST
                    s = npick % 2
                    u = dve.do(lambda e, s=s, k=k, b=b, a0=a0, n=n: e.tensor_scalar(
                        pick[:, s, 0, 0:n], steps[:, a0:a0 + n], ends[:, 2 * k, b:b + 1], None, ALU.is_le),
                        t_ends, i0, pick_free[s])
                    v = dve.do(lambda e, s=s, k=k, b=b, a0=a0, n=n: e.scalar_tensor_tensor(
                        out=pick[:, s, 1, 0:n], in0=steps[:, a0:a0 + n], scalar=ends[:, 2 * k + 1, b:b + 1],
                        in1=pick[:, s, 0, 0:n], op0=ALU.is_gt, op1=ALU.mult), u)
                    pe.wait(v, psum_free)
                    for i, left in enumerate([tab[:, 0, b, :], tabw[:, k, b, :], tab[:, 2, b, :], tcol[:, b:b + 1]]):
                        m = left.shape[1]
                        f = lambda e, i=i, left=left, m=m, s=s, n=n, b=b, r=rws: e.matmul(
                            bank[i][0:m, 0:n], left[0:r, :], pick[0:r, s, 1, 0:n], start=(b == 0), stop=(b == TB - 1))
                        if i < 3:
                            pe.quiet(f)
                        else:
                            w = pe.do(f)
                    pick_free[s] = w
                    npick += 1
                a = dve.do(lambda e, n=n: e.tensor_copy(exp_i[:, 0, 0:n], bank[0][:, 0:n]), w, dve.last())
                W = (WA, WR)[k]
                b_ = dve.do(lambda e, n=n, a0=a0, W=W: e.scalar_tensor_tensor(
                    out=exp_f[:, 0, 0:n], in0=steps[:, a0:a0 + n], scalar=-float(W), in1=bank[1][:, 0:n],
                    op0=ALU.mult, op1=ALU.add), a)
                c_ = dve.do(lambda e, n=n: e.tensor_scalar(exp_f[:, 1, 0:n], exp_f[:, 0, 0:n], 0.0, None, ALU.is_ge), b_)
                c_ = dve.do(lambda e, n=n, W=W: e.scalar_tensor_tensor(
                    out=exp_f[:, 2, 0:n], in0=exp_f[:, 0, 0:n], scalar=float(W), in1=exp_f[:, 1, 0:n],
                    op0=ALU.is_lt, op1=ALU.mult), c_)
                wt = dve.do(lambda e, n=n, a0=a0: e.scalar_tensor_tensor(
                    out=wrow[:, 0:n], in0=bank[3][0:1, 0:n], scalar=-1.0, in1=steps[0:1, a0:a0 + n],
                    op0=ALU.mult, op1=ALU.add), c_)
                if k == 0:
                    lo = dve.do(lambda e, n=n: e.tensor_scalar(exp_i[:, 1, 0:n], exp_i[:, 0, 0:n], P - 1, None,
                                                               ALU.bitwise_and), wt)
                    hi = dve.do(lambda e, n=n: e.tensor_scalar(exp_i[:, 2, 0:n], exp_i[:, 0, 0:n], ROW_LOG2, None,
                                                               ALU.logical_shift_right), lo)
                    psum_free = hi
                    dve.do(lambda e, n=n, a0=a0: e.tensor_copy(slo[:, a0:a0 + n], exp_i[:, 1, 0:n]), hi)
                    g = dve.do(lambda e, n=n: e.scalar_tensor_tensor(
                        out=exp_f[:, 3, 0:n], in0=exp_i[:, 2, 0:n], scalar=float(WA), in1=exp_f[:, 0, 0:n],
                        op0=ALU.mult, op1=ALU.add), hi)
                    g = dve.do(lambda e, n=n: e.scalar_tensor_tensor(
                        out=exp_f[:, 1, 0:n], in0=exp_f[:, 3, 0:n], scalar=1.0, in1=exp_f[:, 2, 0:n],
                        op0=ALU.add, op1=ALU.mult), g)
                    g = dve.do(lambda e, n=n, a0=a0: e.tensor_scalar(code[:, a0:a0 + n], exp_f[:, 1, 0:n], -1.0, None,
                                                                     ALU.add), g)
                    dve.do(lambda e, n=n, a0=a0: e.tensor_scalar(wcol[:, a0:a0 + n], wrow[:, 0:n], float(WA), None,
                                                                 ALU.mult), g)
                else:
                    g = dve.do(lambda e, n=n: e.tensor_copy(exp_f[:, 3, 0:n], bank[2][:, 0:n]), wt)
                    psum_free = g
                    x1 = dve.do(lambda e, n=n: e.tensor_copy(out_i[:, 0, 0:n], exp_i[:, 0, 0:n]), g, store_free)
                    dve.do(lambda e, n=n: e.scalar_tensor_tensor(
                        out=out_i[:, 1, 0:n], in0=exp_i[:, 0, 0:n], scalar=float(REL), in1=exp_f[:, 3, 0:n],
                        op0=ALU.mult, op1=ALU.add), x1)
                    g = dve.do(lambda e, n=n: e.scalar_tensor_tensor(
                        out=exp_f[:, 1, 0:n], in0=exp_f[:, 0, 0:n], scalar=float(REL), in1=exp_f[:, 3, 0:n],
                        op0=ALU.mult, op1=ALU.add), g)
                    g = dve.do(lambda e, n=n: e.scalar_tensor_tensor(
                        out=exp_f[:, 3, 0:n], in0=exp_f[:, 1, 0:n], scalar=1.0, in1=exp_f[:, 2, 0:n],
                        op0=ALU.add, op1=ALU.mult), g)
                    dve.do(lambda e, n=n: e.tensor_scalar(out_c[:, 0:n], exp_f[:, 3, 0:n], -1.0, None, ALU.add), g)
                    g = dve.do(lambda e, n=n: e.tensor_copy(wrow_i[:, 0:n], wrow[:, 0:n]), g)
                    sp.dma(scr_i[:, :, a0:a0 + n], out_i[:, :, 0:n], ch_s, g)
                    sp.dma(scr_c[:, a0:a0 + n], out_c[:, 0:n], ch_s)
                    store_free = sp.dma(scr_w[:, a0:a0 + n], wrow_i[:, 0:n], ch_s)
        t_plan = dve.last()
        cut = carved[0] * 2 // 3
        t_zero = [pool.do(lambda e: e.memset(flat[:, cut:carved[0]], 0.0), t_plan, store_free),
                  dve.do(lambda e: e.memset(flat[:, 0:cut], 0.0), t_plan, store_free, pe.last()), t_zero_rest]

        NL = 8
        iota = sb("iota", [P, 2 * P], F16, own)
        lo_hot = sb("lo_hot", [P, NL, P], F16, own)
        hi_hot = sb("hi_hot", [P, NL, NB * WA], F16, own)
        t_iota = pool.do(lambda e: e.iota(iota[:, :], pattern=[[1, 2 * P]], base=0, channel_multiplier=0,
                                          allow_small_or_imprecise_dtypes=True), t_plan, store_free)
        regs = {}
        mm_tok, lo_tok, hi_tok, add_tok = [], [], [], []

        def hots(j):
            s = j % NL
            free = mm_tok[j - NL] if j >= NL else None
            lo_tok.append(pool.do(lambda e: e.tensor_scalar(lo_hot[:, s, :], iota[:, 0:P], slo[:, j:j + 1], None,
                                                            ALU.is_equal), t_iota, t_plan, free))
            hi_tok.append(dve.do(lambda e: e.tensor_scalar(hi_hot[:, s, :], iota[:, 0:NB * WA], code[:, j:j + 1], None,
                                                           ALU.is_equal), t_iota, t_plan, free))

        for j in range(AHEAD):
            hots(j)
        for j in range(JA):
            s = j % NL
            mm_tok.append(pe.do(lambda e, s=s, j=j: e.matmul(bank[4 + j % 4][:, 0:NB * WA], lo_hot[:, s, :],
                                                             hi_hot[:, s, :], start=True, stop=True),
                                lo_tok[j], hi_tok[j], add_tok[j - 4] if j >= 4 else None))
            if j % REGS == 0:
                n = min(REGS, JA - j)

                def load(e, j=j, n=n):
                    if not regs:
                        regs["dve"] = [e.alloc_register(f"window{i}") for i in range(REGS)]
                    e.load(regs["dve"][0:n], wcol[0:1, j:j + n])
                dve.quiet(load)

            def add(e, j=j):
                c = e.snap(regs["dve"][j % REGS], min_val=0, max_val=NP - WA)
                a = adj[:, :, bass.ds(c, WA)]
                return e.tensor_tensor(a, a, bank[4 + j % 4][:, 0:NB * WA].rearrange("p (h w) -> p h w", w=WA), ALU.add)
            add_tok.append(dve.do(add, mm_tok[j], add_tok[j - 1] if j else None, *t_zero))
            if j + AHEAD < JA:
                hots(j + AHEAD)
        own.close()
        for b in range(NB):
            t_self = dve.do(lambda e, b=b: e.tensor_tensor(adj[:, b, b * P:b * P + P], adj[:, b, b * P:b * P + P],
                                                           ident16[:, :], ALU.add), add_tok[-1], t_ident)
        adj_ready = t_self

        dense = ExitStack()
        split = sb("split", [P, NB, 2, D], F16, dense)
        hT = split[:, :, :, :].rearrange("p b s d -> p (b s d)").bitcast(F32)
        weights = sb("weights", [P, 7, D], F32, dense)
        deg = sb("deg", [P, NB], F32, dense)
        dinv = sb("dinv", [P, NB], F32, dense)
        ch_w = channel("ch_weights")
        WT = {}
        for k, name in enumerate(["L0_gnn_W1", "L0_gnn_W2", "L0_gnn_W3", "L1_gnn_W", "L2_gnn_W1", "L2_gnn_W2"]):
            WT[name] = weights[:, k, :]
            t_w = sp.dma(weights[:, k, :], io[name], ch_w, t_self)

        def turn(ready):
            token = ready
            k = 0
            freed = [None] * 8
            ends_ = []
            pairs = []
            for i in range(NB):
                pairs.append((i, i, 1))
                for j0 in range(i + 1, NB, 8):
                    pairs.append((i, j0, min(8, NB - j0)))
            for i, j0, n in pairs:
                pa, pb = (2 * k) % 8, (2 * k + 1) % 8
                k += 1
                va = bank[pa][:, :].bitcast(F16)
                vb = bank[pb][:, :].bitcast(F16)
                pe.wait(token, t_ident, freed[pa], freed[pb])
                for m in range(n):
                    j = j0 + m
                    f = lambda e, m=m, j=j, i=i, va=va: e.transpose(va[:, m * P:m * P + P], adj[:, i, j * P:j * P + P], ident16[:, :])
                    if m == n - 1:
                        w1 = pe.do(f)
                    else:
                        pe.quiet(f)
                w2 = w1
                if j0 != i:
                    for m in range(n):
                        j = j0 + m
                        f = lambda e, m=m, j=j, i=i, vb=vb: e.transpose(vb[:, m * P:m * P + P], adj[:, j, i * P:i * P + P], ident16[:, :])
                        if m == n - 1:
                            w2 = pe.do(f)
                        else:
                            pe.quiet(f)
                freed[pa] = act.do(lambda e, i=i, j0=j0, n=n, va=va: e.activation(
                    adj[:, j0:j0 + n, i * P:i * P + P], va[:, 0:n * P].rearrange("p (n q) -> p n q", q=P), ACT.Copy), w2)
                ends_.append(freed[pa])
                if j0 != i:
                    freed[pb] = dve.do(lambda e, i=i, j0=j0, n=n, vb=vb: e.tensor_copy(
                        adj[:, i, j0 * P:(j0 + n) * P], vb[:, 0:n * P]), w2)
                    ends_.append(freed[pb])
            return [act.last(), dve.last()]

        def degrees(ready, to):
            pe.wait(*ready, t_const)
            for b in range(NB):
                for k in range(NB):
                    f = lambda e, b=b, k=k: e.matmul(bank[7][:, b:b + 1], adj[:, k, b * P:b * P + P], ones16[:, :],
                                                     start=(k == 0), stop=(k == NB - 1))
                    if b == NB - 1 and k == NB - 1:
                        w = pe.do(f)
                    else:
                        pe.quiet(f)
            return dve.do(lambda e: e.tensor_copy(to[:, :], bank[7][:, 0:NB]), w)

        def aggregate(ready, unscale, eps_rhs=None):
            pe.wait(*ready)
            for k in range(NB):
                for s in range(2):
                    for c, (c0, n) in enumerate(chunk):
                        last = k == NB - 1 and s == 1
                        f = lambda e, k=k, s=s, c=c, c0=c0, n=n, last=last: e.matmul(
                            bank[c][:, 0:n], split[:, k, s, :], adj[:, k, c0:c0 + n],
                            start=(k == 0 and s == 0), stop=last)
                        if last and c == NCH - 1:
                            w = pe.do(f)
                        else:
                            pe.quiet(f)
                    if eps_rhs is not None and k == 0 and s == 0:
                        for b in range(NB):
                            pe.quiet(lambda e, b=b: e.matmul(
                                bank[b * P // CH][:, b * P % CH:b * P % CH + P], xres[:, b, :], eps_rhs,
                                start=False, stop=False, skip_group_check=True))
            toks = []
            for c, (c0, n) in enumerate(chunk):
                if c % 2:
                    toks.append(dve.do(lambda e, c=c, c0=c0, n=n: e.tensor_scalar(zT[:, c0:c0 + n], bank[c][:, 0:n],
                                                                                 unscale, None, ALU.mult), w))
                else:
                    toks.append(act.do(lambda e, c=c, c0=c0, n=n: e.activation(zT[:, c0:c0 + n], bank[c][:, 0:n],
                                                                               ACT.Copy if isinstance(unscale, float) else ACT.Identity,
                                                                               scale=unscale), w))
            return toks

        def project(ready, W, fold):
            token = None
            pe.wait(*ready)
            for b in range(NB):
                c, o = b // 4 % 7, b % 4 * P
                w = pe.do(lambda e, b=b, c=c, o=o: e.matmul(bank[c][:, o:o + P], zT[:, b * P:b * P + P], W,
                                                            start=True, stop=True))
                if b % 4 == 3 or b == NB - 1:
                    for bb in range(b // 4 * 4, b + 1):
                        token = fold(bb, bank[bb // 4 % 7][:, bb % 4 * P:bb % 4 * P + P], w)
            return token

        def rsqrt(to, var, eps, ready):
            n = to.shape[1]
            v, r = root[:, 0, 0:n], root[:, 1, 0:n]
            a = dve.do(lambda e: e.tensor_scalar(v, var, eps, None, ALU.add), ready)
            a = act.do(lambda e: e.activation(r, v, ACT.Sqrt), a)
            a = dve.do(lambda e: e.reciprocal(to, r), a)
            a = dve.do(lambda e: e.tensor_tensor(r, to, to, ALU.mult), a)
            a = dve.do(lambda e: e.tensor_tensor(r, r, v, ALU.mult), a)
            a = dve.do(lambda e: e.tensor_scalar(r, r, -0.5, 1.5, ALU.mult, ALU.add), a)
            return dve.do(lambda e: e.tensor_tensor(to, to, r, ALU.mult), a)

        def norm_stats(src, ready):
            for b in range(NB):
                a = dve.do(lambda e, b=b: e.bn_stats(stats[:, b, :], src[:, b, :]), *ready)
            for b in range(NB):
                c = dve.do(lambda e, b=b: e.bn_aggr(mv[:, b, :], stats[:, b, :]), a)
            d = rsqrt(rstd[:, :], mv[:, :, 1], EPS, c)
            return dve.do(lambda e: e.scalar_tensor_tensor(out=nmr[:, :], in0=mv[:, :, 0], scalar=-1.0, in1=rstd[:, :],
                                                           op0=ALU.mult, op1=ALU.mult), d)

        def normalize(dst, src, ready):
            t = norm_stats(src, ready)
            for b in range(NB):
                if b % 3 == 0:
                    dve.do(lambda e, b=b: e.tensor_scalar(dst[:, b, :], src[:, b, :], rstd[:, b:b + 1],
                                                          nmr[:, b:b + 1], ALU.mult, ALU.add), t)
                else:
                    act.do(lambda e, b=b: e.activation(dst[:, b, :], src[:, b, :], ACT.Identity,
                                                       bias=nmr[:, b:b + 1], scale=rstd[:, b:b + 1]), t)
            return [dve.last(), act.last()]

        def bcast(row):
            return row.unsqueeze(1).broadcast_to([P, NB, D])

        def percol(col):
            return col.unsqueeze(2).broadcast_to([P, NB, D])

        def split_fixed(ready):
            a = act.do(lambda e: e.activation(split[:, :, 0, :], xres[:, :, :], ACT.Copy, scale=FX), *ready)
            return [dve.do(lambda e: e.scalar_tensor_tensor(out=split[:, :, 1, :], in0=xres[:, :, :], scalar=FX,
                                                            in1=split[:, :, 0, :], op0=ALU.mult, op1=ALU.subtract), a)]

        turned = turn(adj_ready)
        t_deg = degrees(turned, deg)
        t_dinv = rsqrt(dinv[:, :], deg[:, :], 0.0, t_deg)

        src_nodes, ready = xres, [t_x]
        for layer in (1, 2, 3):
            W, bias = WT[f"L0_gnn_W{layer}"], ROW[f"L0_gnn_b{layer}"]
            gain, beta = ROW[f"L0_gnn_g{layer}"], ROW[f"L0_gnn_beta{layer}"]
            a = dve.do(lambda e, s=src_nodes: e.tensor_tensor(znode, s[:, :, :], percol(dinv[:, :]), ALU.mult),
                       t_dinv, *ready)
            b = dve.do(lambda e: e.tensor_reduce(small[:, 0:1], zT[:, :], AX.X, ALU.max, apply_absolute_value=True), a)
            c = pool.do(lambda e: e.partition_all_reduce(small[:, 1:2], small[:, 0:1], P, bass.bass_isa.ReduceOp.max), b)
            d = dve.do(lambda e: e.tensor_scalar(small[:, 2:3], small[:, 1:2], 2.0 ** -100, 2.0 ** 110, ALU.max, ALU.min), c)
            d = dve.do(lambda e: e.tensor_scalar(smalli[:, 0:1], small[:, 2:3].bitcast(I32), 0x7F800000, None,
                                                 ALU.bitwise_and), d)
            d = dve.do(lambda e: e.tensor_scalar(small[:, 3:4], smalli[:, 0:1].bitcast(F32), 2.0 ** -14, None, ALU.mult), d)
            d = dve.do(lambda e: e.reciprocal(small[:, 4:5], small[:, 3:4]), d)
            f = act.do(lambda e: e.activation(split[:, :, 0, :], znode, ACT.Identity, scale=small[:, 4:5]), d)
            g = dve.do(lambda e: e.scalar_tensor_tensor(out=split[:, :, 1, :], in0=znode, scalar=small[:, 4:5],
                                                        in1=split[:, :, 0, :], op0=ALU.mult, op1=ALU.subtract), f)
            z = aggregate([g, *turned], small[:, 3:4])

            def fold(b, ps, w, bias=bias):
                return dve.do(lambda e: e.scalar_tensor_tensor(out=znode[:, b, :], in0=ps, scalar=dinv[:, b:b + 1],
                                                               in1=bias, op0=ALU.mult, op1=ALU.add), w)
            h = project([*z, t_w], W, fold) if layer > 1 else project([*z, t_w], W, (lambda fold: lambda b, ps, w: (dve.wait(t_param), fold(b, ps, w))[1])(fold))
            n = normalize(znode, znode, [h])
            a = dve.do(lambda e, g=gain: e.tensor_tensor(znode, znode, bcast(g), ALU.mult), *n)
            a = dve.do(lambda e, g=beta: e.tensor_tensor(znode, znode, bcast(g), ALU.add), a)
            if layer < 3:
                a = dve.do(lambda e: e.tensor_scalar(znode, znode, 0.0, None, ALU.max), a)
            else:
                a = dve.do(lambda e: e.scalar_tensor_tensor(out=znode, in0=znode, scalar=0.0, in1=xres[:, :, :],
                                                            op0=ALU.max, op1=ALU.add), a)
            src_nodes, ready = znode, [a]
        x_ready = normalize(xres, znode, ready)

        sp_ready = split_fixed(x_ready)
        back = turn(h)
        t_cnt = degrees(back, deg)
        z = aggregate([*sp_ready, *back], 1.0 / FX)
        tr = pe.do(lambda e: e.transpose(bank[7][:, 0:P], WT["L1_gnn_W"], ident[:, :]), t_cnt)
        tr = dve.do(lambda e: e.tensor_copy(weights[:, 6, :], bank[7][:, 0:P]), tr)

        def fold1(b, ps, w):
            a = dve.do(lambda e: e.scalar_tensor_tensor(out=znode[:, b, :], in0=ROW["L1_gnn_b"], scalar=deg[:, b:b + 1],
                                                        in1=ps, op0=ALU.mult, op1=ALU.add), w, t_cnt)
            return a
        h = project([*z, tr], weights[:, 6, :], fold1)
        h = dve.do(lambda e: e.tensor_tensor(znode, znode, xres[:, :, :], ALU.add), h)
        x_ready = normalize(xres, znode, [h])

        sp_ready = split_fixed(x_ready)
        eps_id = weights[:, 6, :]
        ei = dve.do(lambda e: e.tensor_scalar(eps_id, ident[:, :], colp[:, 10:11], FX, ALU.mult, ALU.mult), h, t_param)
        z = aggregate([*sp_ready, *x_ready, ei], 1.0 / FX, eps_id)
        adj_free = pe.last()
        cur, nxt = zT[:, :], hT
        ready = z
        bstat = stats[:, 0:NCH, :]
        for layer in (1, 2):
            W = WT[f"L2_gnn_W{layer}"]
            b_, g_, be_ = (COL[f"L2_gnn_{n}{layer}"] for n in ("b", "g", "beta"))
            pe.wait(*ready)
            toks = []
            for c, (c0, n) in enumerate(chunk):
                w = pe.do(lambda e, c=c, c0=c0, n=n, cur=cur, W=W: e.matmul(bank[c][:, 0:n], W, cur[:, c0:c0 + n],
                                                                           start=True, stop=True))
                a = act.do(lambda e, c=c, c0=c0, n=n, nxt=nxt, b_=b_: e.activation(nxt[:, c0:c0 + n], bank[c][:, 0:n],
                                                                                   ACT.Identity, bias=b_, scale=1.0), w, t_param)
                m = min(n, N - c0)
                a = dve.do(lambda e, c=c, c0=c0, m=m, nxt=nxt: e.bn_stats(bstat[:, c, :], nxt[:, c0:c0 + m]), a)
            a = dve.do(lambda e: e.bn_aggr(mv[:, 0, :], bstat), a)
            a = rsqrt(small[:, 5:6], mv[:, 0, 1:2], EPS, a)
            a = dve.do(lambda e, g_=g_: e.tensor_tensor(small[:, 6:7], small[:, 5:6], g_, ALU.mult), a)
            a = dve.do(lambda e: e.tensor_tensor(small[:, 7:8], mv[:, 0, 0:1], small[:, 6:7], ALU.mult), a)
            a = dve.do(lambda e, be_=be_: e.tensor_tensor(small[:, 8:9], be_, small[:, 7:8], ALU.subtract), a)
            half = 4 * CH
            r1 = act.do(lambda e, nxt=nxt: e.activation(nxt[:, 0:half], nxt[:, 0:half], ACT.Relu, bias=small[:, 8:9],
                                                        scale=small[:, 6:7]), a)
            r2 = act.do(lambda e, nxt=nxt: e.activation(nxt[:, half:NP], nxt[:, half:NP], ACT.Relu, bias=small[:, 8:9],
                                                        scale=small[:, 6:7]), a)
            cur, nxt = nxt, cur
            ready = [r1, r2]
        toks = []
        for b in range(NB):
            c, o = b // 4 % 7, b % 4 * P
            w = pe.do(lambda e, b=b, c=c, o=o, cur=cur: e.transpose(bank[c][:, o:o + P], cur[:, b * P:b * P + P], ident[:, :]),
                      *ready)
            if b % 4 == 3 or b == NB - 1:
                b0 = b // 4 * 4
                n = b + 1 - b0
                toks = dve.do(lambda e, b0=b0, n=n: e.tensor_tensor(
                    xres[:, b0:b0 + n, :], xres[:, b0:b0 + n, :],
                    bank[b0 // 4 % 7][:, 0:n * P].rearrange("p (b d) -> p b d", d=P), ALU.add), w)
        x_ready = normalize(xres, xres, [toks])
        dense.close()
        adj_ctx.close()

        rel = ExitStack()
        sums = sb("sums", [P, NW4, G, D + 1], F32, rel)
        NG = 6
        gath = sb("gath", [P, NG, 3 * D + 1], BF16, rel)
        hot = sb("hot", [P, NG, G * P], BF16, rel)
        iota_r = sb("iota_r", [P, G * P], F16, rel)
        index = sb("index", [P, 2, JR], I32, rel)
        code_r = sb("code_r", [P, JR], F32, rel)
        win = sb("win", [1, JR], I32, rel)
        place = sb("place", [P, REL, P], F32, rel)
        inv = sb("inv", [P, NW4 * G], F32, rel)
        w1 = sb("w1", [P, REL, H], F32, rel)
        root1 = sb("root1", [P, H], F32, rel)
        w2 = sb("w2", [P, HB, REL, D], F32, rel)
        root2 = sb("root2", [P, HB, D], F32, rel)
        parts = sb("parts", [P, 2, REL, 3, D], BF16, rel)
        rest = sb("rest", [P, REL * D], F32, rel)
        relT = sb("relT", [P, 2, REL, P], F32, rel)
        hTr = sb("hTr", [P, 2, HB, P], F32, rel)
        xT = sb("xT", [P, 2, P], F32, rel)
        free_mem = [adj_free, dve.last(), act.last(), pe.last()]

        ch_l3, ch_l4 = channel("ch_l3"), channel("ch_l4")
        sp.wait(*free_mem, store_free)
        sp.dma(index[:, :, :], scr_i, ch_l3)
        sp.dma(code_r[:, :], scr_c, ch_l3)
        t_lists = sp.dma(win[:, :], scr_w, ch_l3)
        sp.dma(w1[:, :, :], io["L3_gnn_W1"].rearrange("r k o -> k r o"), ch_l4)
        sp.dma(root1[:, :], io["L3_gnn_root1"], ch_l4)
        for h in range(HB):
            sp.dma(w2[:, h, :, :], io["L3_gnn_W2"][:, h * P:h * P + P, :].rearrange("r k o -> k r o"), ch_l4)
        t_w3 = sp.dma(root2[:, :, :], io["L3_gnn_root2"].rearrange("(h k) o -> k h o", k=P), ch_l4)

        pool.wait(*free_mem)
        z0 = pool.do(lambda e: e.memset(gath[:, :, :], 1.0))
        z0 = pool.do(lambda e: e.iota(iota_r[:, :], pattern=[[1, G * P]], base=0, channel_multiplier=0,
                                      allow_small_or_imprecise_dtypes=True))
        z1 = pool.do(lambda e: e.memset(place[:, :, :], 1.0))
        z1 = pool.do(lambda e: e.affine_select(out=place[:, :, :], in_=place[:, :, :], compare_op=ALU.is_ge, fill=0.0,
                                               base=0, pattern=[[REL * GN, P // GN], [-REL, P]], channel_multiplier=1), z1)
        t_place = pool.do(lambda e: e.affine_select(out=place[:, :, :], in_=place[:, :, :], compare_op=ALU.is_ge, fill=0.0,
                                                    base=REL - 1, pattern=[[-REL * GN, P // GN], [REL, P]],
                                                    channel_multiplier=-1), z1)
        half_w = NW4 // 2
        z2 = pool.do(lambda e: e.memset(sums[:, half_w:NW4, :, :], 0.0))
        z3 = dve.do(lambda e: e.memset(sums[:, 0:half_w, :, :], 0.0), *free_mem)
        sums_zero = [z2, z3]

        def three_parts(dst3, src, scratch, ready, n):
            a = act.do(lambda e: e.activation(dst3(0), src, ACT.Copy), *ready)
            a = dve.do(lambda e: e.tensor_tensor(scratch, src, dst3(0), ALU.subtract), a)
            b = act.do(lambda e: e.activation(dst3(1), scratch, ACT.Copy), a)
            b = dve.do(lambda e: e.tensor_tensor(dst3(2), scratch, dst3(1), ALU.subtract), b)
            return b

        ch_t1 = channel("ch_table1")
        part_free = [None, None]
        NBH = REL
        for i, b0 in enumerate(range(0, NB, NBH)):
            n = min(NBH, NB - b0)
            s = i % 2
            scratch = rest[:, 0:n * D].rearrange("p (b d) -> p b d", d=D)
            t = three_parts(lambda q, s=s, n=n: parts[:, s, 0:n, q, :], xres[:, b0:b0 + n, :], scratch,
                            [*x_ready, *free_mem, part_free[s]], n)
            part_free[s] = sp.dma(table1[b0 * P:(b0 + n) * P, :].rearrange("(b p) f -> p b f", p=P),
                                  parts[:, s, 0:n, :, :].rearrange("p b q d -> p b (q d)"), ch_t1, t)
            dve.wait(part_free[s])
        t_table1 = part_free[(len(range(0, NB, NBH)) - 1) % 2]

        ch_g = [channel(f"ch_gather{i}") for i in range(NG)]
        dregs = {"r": None}

        def relation_sums(table, which, ready):
            gt, ht, mt, at = [], [], [], []
            pool.wait(*ready, t_lists, z0)
            dve.wait(*sums_zero, t_lists, z0)

            def gather(j):
                s = j % NG
                ch = ch_g[s]
                ch[1] += 16
                pool.wait(mt[j - NG] if j >= NG else None)
                pool.program.append(lambda e, s=s, j=j: e.indirect_dma_start(
                    gath[:, s, 0:3 * D], None, table,
                    bass.IndirectOffsetOnAxis(ap=index[:, which, j:j + 1].bitcast(U32), axis=0)).then_inc(ch_g[s][0], 16))
                gt.append((ch[0], ch[1]))

            def one_hot(j):
                s = j % NG
                ht.append(dve.do(lambda e, s=s, j=j: e.tensor_scalar(hot[:, s, :], iota_r[:, :], code_r[:, j:j + 1], None,
                                                                     ALU.is_equal), mt[j - NG] if j >= NG else None))

            for j in range(AHEAD):
                one_hot(j)
            for j in range(JR):
                s = j % NG
                gather(j)
                pe.wait(gt[j], ht[j], at[j - 4] if j >= 4 else None)
                ps = bank[j % 4]
                for g in range(G):
                    for q, (a, b) in enumerate([(2 * D, 3 * D + 1), (D, 2 * D), (0, D)]):
                        f = lambda e, g=g, q=q, a=a, b=b, s=s, ps=ps: e.matmul(
                            ps[:, g * (D + 1):g * (D + 1) + b - a], hot[:, s, g * P:g * P + P], gath[:, s, a:b],
                            start=(q == 0), stop=(q == 2), skip_group_check=True)
                        if g == G - 1 and q == 2:
                            m = pe.do(f)
                        else:
                            pe.quiet(f)
                mt.append(m)
                if j % REGS == 0:
                    n = min(REGS, JR - j)

                    def load(e, j=j, n=n):
                        dregs["r"] = regs["dve"]
                        e.load(dregs["r"][0:n], win[0:1, j:j + n])
                    dve.quiet(load)

                def add(e, j=j, ps=ps):
                    c = e.snap(dregs["r"][j % REGS], min_val=0, max_val=NW4 - 1)
                    a = sums[:, bass.ds(c, 1), :, :].rearrange("p o g d -> p (o g d)")
                    return e.tensor_tensor(a, a, ps[:, 0:G * (D + 1)], ALU.add)
                if j:
                    prev = at[j - 1]
                else:
                    prev = None
                at.append(dve.do(add, mt[j], prev))
                if j + AHEAD < JR:
                    one_hot(j + AHEAD)
            cnt = sums[:, :, :, D].rearrange("p w g -> p (w g)")
            a = dve.do(lambda e: e.tensor_scalar(inv[:, :], cnt, 1.0, None, ALU.max), at[-1])
            return dve.do(lambda e: e.reciprocal(inv[:, :], inv[:, :]), a)

        GB = WPB * G
        sums_g = sums[:, :, :, :].rearrange("p w g d -> p (w g) d")

        done = relation_sums(table1, 0, [t_table1])
        root_out = znode
        ch_t2 = [channel(f"ch_table2_{i}") for i in range(2)]
        relT_free, hT_free = [None, None], [None, None]
        b7 = None
        bank_free = [None] * 8
        zero_tok = None
        pe.wait(t_w3)
        part_free = [part_free[0], part_free[1]]
        for nb in range(NB):
            s = nb % 2
            g0 = nb * GB
            a = dve.do(lambda e, g0=g0: e.tensor_tensor(
                sums_g[:, g0:g0 + GB, 0:D], sums_g[:, g0:g0 + GB, 0:D],
                inv[:, g0:g0 + GB].unsqueeze(2).broadcast_to([P, GB, D]), ALU.mult), done)
            for h in range(2):
                pe.wait(a, bank_free[h])
                for q in range(4):
                    m = pe.do(lambda e, h=h, q=q, g0=g0: e.transpose(bank[h][:, q * P:q * P + P],
                                                                    sums_g[:, g0 + 4 * h + q, 0:D], ident[:, :]))
                bank_free[h] = act.do(lambda e, h=h, s=s: e.activation(
                    relT[:, s, :, h * 4 * GN:(h + 1) * 4 * GN].rearrange("p r n -> p n r"),
                    bank[h][:, :].rearrange("p (n r) -> p n r", r=REL), ACT.Copy), m, relT_free[s])
            m_turn = m
            zero_tok = pool.do(lambda e, g0=g0: e.memset(sums_g[:, g0:g0 + GB, :], 0.0), m_turn, done)
            m = pe.do(lambda e, nb=nb: e.transpose(bank[2][:, 0:P], xres[:, nb, :], ident[:, :]), bank_free[2], *x_ready)
            t_xT = bank_free[2] = act.do(lambda e, s=s: e.activation(xT[:, s, :], bank[2][:, 0:P], ACT.Copy), m, relT_free[s])
            pe.wait(bank_free[0], bank_free[1], t_xT, bank_free[3])
            for o in range(HB):
                for r in range(REL):
                    pe.quiet(lambda e, o=o, r=r, s=s: e.matmul(bank[3][:, o * P:o * P + P], w1[:, r, o * P:o * P + P],
                                                               relT[:, s, r, :], start=(r == 0), stop=False,
                                                               skip_group_check=True))
                m = pe.do(lambda e, o=o, s=s: e.matmul(bank[3][:, o * P:o * P + P], root1[:, o * P:o * P + P],
                                                       xT[:, s, :], start=False, stop=True, skip_group_check=True))
            relT_free[s] = m
            for o in range(HB):
                bank_free[3] = act.do(lambda e, o=o, s=s: e.activation(hTr[:, s, o, :], bank[3][:, o * P:o * P + P],
                                                                       ACT.Relu, bias=colp[:, 8 + o:9 + o], scale=1.0),
                                      m, hT_free[s])
            pe.wait(bank_free[3], bank_free[4], bank_free[5], bank_free[6])
            for y in range(2):
                for k in range(HB):
                    pe.quiet(lambda e, y=y, k=k, s=s: e.matmul(
                        bank[4 + y][:, :], hTr[:, s, k, :], w2[:, k, 4 * y:4 * y + 4, :].rearrange("p r d -> p (r d)"),
                        start=(k == 0), stop=(k == HB - 1)))
            for k in range(HB):
                m = pe.do(lambda e, k=k, s=s: e.matmul(bank[6][:, 0:P], hTr[:, s, k, :], root2[:, k, :],
                                                       start=(k == 0), stop=(k == HB - 1)))
            hT_free[s] = m
            a = dve.do(lambda e, nb=nb: e.tensor_tensor(root_out[:, nb, :], bank[6][:, 0:P], ROW["L3_gnn_b2"], ALU.add), m, *x_ready)
            bank_free[6] = a
            for y in range(2):
                scratch = rest[:, y * CH:(y + 1) * CH].rearrange("p (r d) -> p r d", d=D)
                t = three_parts(lambda q, s=s, y=y: parts[:, s, 4 * y:4 * y + 4, q, :],
                                bank[4 + y][:, :].rearrange("p (r d) -> p r d", d=D), scratch,
                                [m, part_free[s]], 4)
                bank_free[4 + y] = t
            part_free[s] = sp.dma(table2[nb * P * REL:(nb + 1) * P * REL, :].rearrange("(p r) f -> p (r f)", r=REL),
                                  parts[:, s, :, :, :].rearrange("p r q d -> p (r q d)"), ch_t2[s], t)
        xr = dve.do(lambda e: e.tensor_tensor(root_out, root_out, xres[:, :, :], ALU.add), dve.last())
        t_table2 = part_free[(NB - 1) % 2]

        sums_zero = [zero_tok]
        done = relation_sums(table2, 1, [t_table2, part_free[0], part_free[1]])
        bf = [None] * 8
        for nb in range(NB):
            g0 = nb * GB
            c = nb % 4
            a = dve.do(lambda e, g0=g0: e.tensor_tensor(
                sums_g[:, g0:g0 + GB, 0:D], sums_g[:, g0:g0 + GB, 0:D],
                inv[:, g0:g0 + GB].unsqueeze(2).broadcast_to([P, GB, D]), ALU.mult), done)
            pe.wait(a, bf[c], t_place)
            for q in range(GB):
                f = lambda e, q=q, g0=g0, c=c: e.matmul(bank[c][:, 0:D], place[:, q, :], sums_g[:, g0 + q, 0:D],
                                                        start=(q == 0), stop=(q == GB - 1))
                m = pe.do(f)
            bf[c] = dve.do(lambda e, nb=nb, c=c: e.tensor_tensor(root_out[:, nb, :], root_out[:, nb, :], bank[c][:, 0:D],
                                                                 ALU.add), m, xr)
        final = normalize(xres, znode, [dve.last()])
        ch_o = channel("ch_out")
        sp.dma(out[0:FULL * P, :].rearrange("(b p) d -> p b d", p=P), xres[:, 0:FULL, :], ch_o, *final)
        t_out = sp.dma(out[FULL * P:N, :], xres[0:TAILN, FULL, :], ch_o)
        sp.wait(t_out)
        rel.close()

        block = ctx.enter_context(nc.Block())

        @block.tensor
        def _(e):
            pe.replay(e)

        @block.vector
        def _(e):
            dve.replay(e)

        @block.scalar
        def _(e):
            act.replay(e)

        @block.gpsimd
        def _(e):
            pool.replay(e)

        @block.sync
        def _(e):
            sp.replay(e)


_INS = ['x', 'src', 'dst', 'edge_type_8'] + [f"L0_gnn_{p}{i}" for i in (1, 2, 3) for p in ("W", "b", "g", "beta")] + \
    ['L1_gnn_W', 'L1_gnn_b', 'L2_gnn_eps', 'L2_gnn_W1', 'L2_gnn_b1', 'L2_gnn_g1', 'L2_gnn_beta1', 'L2_gnn_W2',
     'L2_gnn_b2', 'L2_gnn_g2', 'L2_gnn_beta2', 'L3_gnn_W1', 'L3_gnn_root1', 'L3_gnn_b1', 'L3_gnn_W2',
     'L3_gnn_root2', 'L3_gnn_b2']


def kernel(**inputs):
    import numpy as _np
    import concourse.bacc as _bacc
    from concourse import mybir as _mybir
    from concourse.bass_utils import run_bass_kernel_spmd as _run

    nc = _bacc.Bacc("TRN2", target_bir_lowering=False, num_devices=1)
    arrays, io = {}, {}
    for name in _INS:
        a = _np.ascontiguousarray(inputs[name])
        arrays[f"in_{name}_dram"] = a
        io[name] = nc.dram_tensor(f"in_{name}_dram", a.shape, _mybir.dt.from_np(a.dtype), kind="ExternalInput").ap()
    x = arrays["in_x_dram"]
    out = nc.dram_tensor("out_0_dram", x.shape, _mybir.dt.from_np(x.dtype), kind="ExternalOutput").ap()
    gnn_stack(nc, io, out)
    r = _run(nc, [arrays], core_ids=[0])
    return r.results[0]["out_0_dram"]
```

```python
from contextlib import ExitStack

import concourse.bass as bass
from concourse import mybir

ALU = mybir.AluOpType
ACT = mybir.ActivationFunctionType
AX = mybir.AxisListType
F32 = mybir.dt.float32
F16 = mybir.dt.float16
BF16 = mybir.dt.bfloat16
I32 = mybir.dt.int32
U32 = mybir.dt.uint32

P = 128
EPS = 1e-5
REL = 8
ROW_LOG2 = 7
WA = 8
WA_LOG2 = 3
GA = 2
WR = 32
WR_LOG2 = 5
REGS = 32
AHEAD = 4


class Lane:

    def __init__(self, sem):
        self.sem, self.count, self.program, self.seen = sem, 0, [], {}

    def wait(self, *tokens):
        for token in tokens:
            if token is None:
                continue
            sem, value = token
            if self.seen.get(id(sem), 0) < value:
                self.seen[id(sem)] = value
                self.program.append(lambda e, s=sem, v=value: e.wait_ge(s, v))

    def do(self, emit, *tokens):
        self.wait(*tokens)
        self.count += 1
        self.program.append(lambda e, f=emit, s=self.sem: f(e).then_inc(s, 1))
        return (self.sem, self.count)

    def quiet(self, emit, *tokens):
        self.wait(*tokens)
        self.program.append(lambda e, f=emit: f(e))

    def dma(self, out, in_, channel, *tokens, **how):
        self.wait(*tokens)
        channel[1] += 16
        self.program.append(lambda e, s=channel[0]: e.dma_start(out, in_, **how).then_inc(s, 16))
        return (channel[0], channel[1])

    def last(self):
        return (self.sem, self.count) if self.count else None

    def replay(self, e):
        for step in self.program:
            step(e)


def gnn_stack(nc, io, out):
    N, D = io["x"].shape
    E = io["src"].shape[0]
    NB = -(-N // P)
    NP = NB * P
    FULL = N // P
    TAILN = N - FULL * P
    T = -(-E // P)
    TB = -(-T // P)
    TFULL = (E // P) // P
    TROWS = E // P - TFULL * P
    TREST = E - (E // P) * P
    TLAST = T - TFULL * P
    JA = T + -(-N // WA) - 1
    JR = T + -(-N // WR) - 1
    H = io["L3_gnn_W1"].shape[2]
    HB = H // P
    CH = 512
    NCH = -(-NP // CH)
    chunk = [(c * CH, min(CH, NP - c * CH)) for c in range(NCH)]
    G = WR * REL // P
    GN = P // REL
    NW4 = NB * P // WR
    WPB = P // WR
    FX = 1024.0

    ctx = ExitStack()
    with ctx:
        def sem(name):
            return ctx.enter_context(nc.semaphore(name))

        def channel(name):
            return [sem(name), 0]

        def sb(name, shape, dt, where=None):
            return (where or ctx).enter_context(nc.sbuf_tensor(name, shape, dt))

        pe, dve, act, pool, sp = (Lane(sem(f"s_{n}")) for n in ("pe", "dve", "act", "pool", "sp"))
        bank = [ctx.enter_context(nc.psum_tensor(f"bank{i}", [P, CH], F32)) for i in range(8)]

        ident = sb("ident", [P, P], F32)
        ident16 = sb("ident16", [P, P], F16)
        ones16 = sb("ones16", [P, 1], F16)
        ones_row = sb("ones_row", [1, P], F32)
        xres = sb("xres", [P, NB, D], F32)
        zT = sb("zT", [P, NP], F32)
        znode = zT[:, :].rearrange("p (b d) -> p b d", d=D)
        stats = sb("stats", [P, NB, 6], F32)
        mv = sb("mv", [P, NB, 2], F32)
        rstd = sb("rstd", [P, NB], F32)
        root = sb("root", [P, 2, NB], F32)
        nmr = sb("nmr", [P, NB], F32)
        small = sb("small", [P, 16], F32)
        smalli = sb("smalli", [P, 2], I32)
        rows = sb("rows", [P, 12, D], F32)
        colp = sb("colp", [P, 16], F32)

        scr_w = nc.dram_tensor("scr_windows", [1, JR], I32, kind="Internal").ap()
        scr_i = nc.dram_tensor("scr_index", [P, 2, JR], I32, kind="Internal").ap()
        scr_c = nc.dram_tensor("scr_code", [P, JR], F32, kind="Internal").ap()
        table1 = nc.dram_tensor("table1", [NP, 3 * D], BF16, kind="Internal").ap()
        table2 = nc.dram_tensor("table2", [NP * REL, 3 * D], BF16, kind="Internal").ap()

        m0 = pool.do(lambda e: e.memset(ident[:, :], 0.0))
        m1 = pool.do(lambda e: e.affine_select(out=ident[:, :], in_=ident[:, :], compare_op=ALU.not_equal,
                                               fill=1.0, base=0, pattern=[[-1, P]], channel_multiplier=1), m0)
        t_ident = pool.do(lambda e: e.tensor_copy(ident16[:, :], ident[:, :]), m1)
        pool.do(lambda e: e.memset(ones_row[:, :], 1.0))
        t_const = pool.do(lambda e: e.memset(ones16[:, :], 1.0))

        ch_x, ch_p = channel("ch_x"), channel("ch_param")
        m2 = dve.do(lambda e: e.memset(xres[:, FULL, :], 0.0))
        sp.dma(xres[:, 0:FULL, :], io["x"][0:FULL * P, :].rearrange("(b p) d -> p b d", p=P), ch_x)
        t_x = sp.dma(xres[0:TAILN, FULL, :], io["x"][FULL * P:N, :], ch_x, m2)

        ROW = {}
        for k, name in enumerate(["L0_gnn_b1", "L0_gnn_g1", "L0_gnn_beta1", "L0_gnn_b2", "L0_gnn_g2",
                                  "L0_gnn_beta2", "L0_gnn_b3", "L0_gnn_g3", "L0_gnn_beta3", "L1_gnn_b",
                                  "L3_gnn_b2"]):
            ROW[name] = rows[:, k, :]
            act.dma(rows[:, k, :], io[name].rearrange("(a d) -> a d", a=1).broadcast_to([P, D]), ch_p)
        COL = {}
        for k, name in enumerate(["L2_gnn_b1", "L2_gnn_g1", "L2_gnn_beta1", "L2_gnn_b2", "L2_gnn_g2",
                                  "L2_gnn_beta2"]):
            COL[name] = colp[:, k:k + 1]
            act.dma(colp[:, k:k + 1], io[name].rearrange("(d a) -> d a", a=1), ch_p)
        for h in range(HB):
            act.dma(colp[:, 8 + h:9 + h], io["L3_gnn_b1"][h * P:h * P + P].rearrange("(d a) -> d a", a=1), ch_p)
        t_param = act.dma(colp[:, 10:11], io["L2_gnn_eps"].rearrange("(a d) -> a d", a=1).broadcast_to([P, 1]), ch_p)

        adj_ctx = ExitStack()
        adj = sb("adj", [P, NB, NP], F16, adj_ctx)
        own = ExitStack()
        flat = adj[:, :, :].rearrange("p b n -> p (b n)").bitcast(F32)
        carved = [0]

        def carve(shape, dt=F32):
            n = 1
            for k in shape[1:]:
                n *= k
            v = flat[0:shape[0], carved[0]:carved[0] + n]
            carved[0] += n
            shape = list(shape)
            if dt == F16:
                shape[-1] *= 2
            if dt != F32:
                v = v.bitcast(dt)
            if len(shape) == 3:
                v = v.rearrange("p (a b) -> p a b", b=shape[2])
            if len(shape) == 4:
                v = v.rearrange("p (a b c) -> p a b c", b=shape[2], c=shape[3])
            return v
        nlo = zT[:, 0:JA]
        code = zT[:, JA:2 * JA]
        wcol = sb("wcol", [1, JA], I32, own)
        tab_i = carve([P, 3, TB, P], I32)
        prev_i = carve([P, TB], I32)
        steps = carve([P, JA])
        steps16 = carve([P, JA // 2], F16)
        ends = carve([P, 4, TB])
        tcol = carve([P, TB])
        tmp_i = carve([P, TB], I32)
        v_i = carve([P, 2, TB, P], I32)
        S_LO, S_HI, TYPE, D_LO, D_HI, TILE = 0, 1, 2, (3, 5), (4, 6), 7
        piece = carve([P, 8, TB, P // 2], F16)
        pick = carve([P, 4, CH // 2], F16)
        exp_f = carve([P, 6, CH])
        out_i = carve([P, 2, CH], I32)
        out_c = carve([P, CH])
        wrow_i = carve([1, CH], I32)
        free_end = NB * NP // 2
        t_zero_rest = pool.do(lambda e: e.memset(flat[:, carved[0]:free_end], 0.0))

        q0 = dve.do(lambda e: e.memset(tab_i[:, :, TFULL, :], 0))
        q1 = dve.do(lambda e: e.memset(tab_i[:, 1, TFULL, :], NP + 4095), q0)
        q2 = dve.do(lambda e: e.memset(prev_i[:, :], 0))
        ch_t = [channel(f"ch_tab{i}") for i in range(3)]
        t_tab = []
        for i, name in enumerate(["src", "dst", "edge_type_8"]):
            e1 = io[name]
            n0 = TFULL * P * P
            sp.dma(tab_i[:, i, 0:TFULL, :], e1[0:n0].rearrange("(b q e) -> q b e", q=P, e=P), ch_t[i])
            sp.dma(tab_i[0:TROWS, i, TFULL, :], e1[n0:n0 + TROWS * P].rearrange("(q e) -> q e", e=P), ch_t[i], q1)
            t_tab.append(sp.dma(tab_i[TROWS:TROWS + 1, i, TFULL, 0:TREST],
                                e1[n0 + TROWS * P:E].rearrange("(q e) -> q e", q=1), ch_t[i]))
        ch_v = channel("ch_prev")
        dst2 = io["dst"][0:(E // P) * P].rearrange("(t e) -> t e", e=P)[:, P - 1:P]
        act.dma(prev_i[1:P, 0:1], dst2[0:P - 1, :], ch_v, q2, allow_slow_non_contiguous=True)
        for b in range(1, TB):
            n = min(P, T - b * P)
            t_prev = act.dma(prev_i[0:n, b:b + 1], dst2[b * P - 1:b * P - 1 + n, :], ch_v,
                             allow_slow_non_contiguous=True)

        i0 = pool.do(lambda e: e.iota(steps[:, :], pattern=[[1, JA]], base=0, channel_multiplier=0,
                                      allow_small_or_imprecise_dtypes=True))
        i1 = pool.do(lambda e: e.iota(tcol[:, :], pattern=[[P, TB]], base=0, channel_multiplier=1,
                                      allow_small_or_imprecise_dtypes=True))
        i2 = dve.do(lambda e: e.tensor_copy(steps16[:, :], steps[:, :]), i0)
        c0 = dve.last()
        dve.wait(i1, t_prev, *t_tab)
        tile3 = tcol[:, :].unsqueeze(2).broadcast_to([P, TB, P])
        dve.do(lambda e: e.tensor_copy(piece[:, TYPE, :, :], tab_i[:, 2, :, :]))
        dve.do(lambda e: e.tensor_copy(piece[:, TILE, :, :], tile3))

        def low_high(v, lo, hi):
            a = dve.do(lambda e: e.tensor_scalar(v_i[:, 1, :, :], v, P - 1, None, ALU.bitwise_and), dve.last())
            dve.do(lambda e: e.tensor_copy(piece[:, lo, :, :], v_i[:, 1, :, :]), a)
            return dve.do(lambda e: e.tensor_tensor(piece[:, hi, :, :], v, v_i[:, 1, :, :], ALU.subtract), a)

        low_high(tab_i[:, 0, :, :], S_LO, S_HI)
        for k, lg in ((0, WA_LOG2), (1, WR_LOG2)):
            a = dve.do(lambda e, lg=lg: e.tensor_scalar(tmp_i[:, :], tab_i[:, 1, :, P - 1], lg, None,
                                                        ALU.logical_shift_right), c0, dve.last())
            a = dve.do(lambda e, k=k: e.tensor_tensor(ends[:, 2 * k, :], tmp_i[:, :], tcol[:, :], ALU.add), a, i1)
            a = dve.do(lambda e, lg=lg: e.tensor_scalar(tmp_i[:, :], prev_i[:, :], lg, None,
                                                        ALU.logical_shift_right), a)
            a = dve.do(lambda e, k=k: e.scalar_tensor_tensor(out=ends[:, 2 * k + 1, :], in0=tmp_i[:, :], scalar=-1.0,
                                                             in1=tcol[:, :], op0=ALU.add, op1=ALU.add), a)
            a = dve.do(lambda e, k=k, W=(WA, WR)[k]: e.scalar_tensor_tensor(
                out=v_i[:, 0, :, :], in0=tile3, scalar=float(W), in1=tab_i[:, 1, :, :], op0=ALU.mult, op1=ALU.add), a)
            low_high(v_i[:, 0, :, :], D_LO[k], D_HI[k])
        t_ends = dve.do(lambda e: e.memset(ends[0:1, 1:4:2, 0:1], -1.0), dve.last())

        plan_done = []
        ch_s = channel("ch_plan")
        pick_free = [None, None]
        psum_free = None
        store_free = None
        npick = 0
        for k, J in ((1, JR), (0, JA)):
            for a0 in range(0, J, CH):
                n = min(CH, J - a0)
                W = (WA, WR)[k]
                if k == 0:
                    sums_of = {0: [S_LO], 1: [S_HI], 2: [D_LO[0], D_HI[0]], 3: [TILE]}
                else:
                    sums_of = {0: [S_LO, S_HI], 1: [TYPE], 2: [D_LO[1], D_HI[1]], 3: [TILE]}
                for b in range(TB):
                    rws = P if b < TFULL else TLAST
                    s = npick % 2
                    u = dve.do(lambda e, s=s, k=k, b=b, a0=a0, n=n: e.tensor_scalar(
                        pick[:, 2 * s, 0:n], steps16[:, a0:a0 + n], ends[:, 2 * k, b:b + 1], None, ALU.is_le),
                        t_ends, i2, pick_free[s])
                    v = dve.do(lambda e, s=s, k=k, b=b, a0=a0, n=n: e.scalar_tensor_tensor(
                        out=pick[:, 2 * s + 1, 0:n], in0=steps16[:, a0:a0 + n], scalar=ends[:, 2 * k + 1, b:b + 1],
                        in1=pick[:, 2 * s, 0:n], op0=ALU.is_gt, op1=ALU.mult), u)
                    pe.wait(v, psum_free)
                    for i, kinds in sums_of.items():
                        for q in kinds:
                            f = lambda e, i=i, q=q, s=s, n=n, b=b, r=rws, kinds=kinds: e.matmul(
                                bank[i][:, 0:n], piece[0:r, q, b, :], pick[0:r, 2 * s + 1, 0:n],
                                start=(b == 0 and q == kinds[0]), stop=(b == TB - 1 and q == kinds[-1]))
                            if q == TILE:
                                w = pe.do(f)
                            else:
                                pe.quiet(f)
                    pick_free[s] = w
                    npick += 1
                st = steps[:, a0:a0 + n]
                PLACE, GE, IN, WIN, X, Y = (exp_f[:, i, 0:n] for i in range(6))
                dve.wait(w, dve.last())
                p_ = dve.do(lambda e, PLACE=PLACE, st=st, W=W, n=n: e.scalar_tensor_tensor(
                    out=PLACE, in0=st, scalar=-float(W), in1=bank[2][:, 0:n], op0=ALU.mult, op1=ALU.add))
                w_ = dve.do(lambda e, WIN=WIN, st=st, n=n: e.scalar_tensor_tensor(
                    out=WIN, in0=bank[3][:, 0:n], scalar=-1.0, in1=st, op0=ALU.mult, op1=ALU.add))
                g_ = dve.do(lambda e, GE=GE, PLACE=PLACE: e.tensor_scalar(GE, PLACE, 0.0, None, ALU.is_ge), p_)
                in_ = dve.do(lambda e, IN=IN, PLACE=PLACE, GE=GE, W=W: e.scalar_tensor_tensor(
                    out=IN, in0=PLACE, scalar=float(W), in1=GE, op0=ALU.is_lt, op1=ALU.mult), g_)
                if k == 0:
                    dve.do(lambda e, n=n, a0=a0: e.tensor_scalar(nlo[:, a0:a0 + n], bank[0][:, 0:n], -1.0, None, ALU.mult))
                    x_ = dve.do(lambda e, n=n, X=X, PLACE=PLACE: e.scalar_tensor_tensor(
                        out=X, in0=bank[1][:, 0:n], scalar=float(WA * GA) / P, in1=PLACE, op0=ALU.mult, op1=ALU.add), in_)
                    psum_free = x_
                    pair = WIN.rearrange("p (a b) -> p a b", b=GA)
                    y_ = dve.do(lambda e, Y=Y, pair=pair, n=n: e.tensor_tensor(
                        Y.rearrange("p (a b) -> p a b", b=GA), pair, pair[:, :, 0:1].broadcast_to([P, n // GA, GA]),
                        ALU.subtract), w_)
                    x_ = dve.do(lambda e, X=X, Y=Y: e.scalar_tensor_tensor(out=X, in0=Y, scalar=float(WA), in1=X,
                                                                           op0=ALU.mult, op1=ALU.add), y_, x_)
                    x_ = dve.do(lambda e, X=X, Y=Y, IN=IN: e.scalar_tensor_tensor(
                        out=Y, in0=X, scalar=1.0, in1=IN, op0=ALU.add, op1=ALU.mult), x_)
                    dve.do(lambda e, Y=Y, a0=a0, n=n: e.tensor_scalar(code[:, a0:a0 + n], Y, -1.0, None, ALU.add), x_)
                    dve.do(lambda e, WIN=WIN, a0=a0, n=n: e.tensor_scalar(wcol[:, a0:a0 + n], WIN[0:1, :], float(WA),
                                                                          None, ALU.mult))
                else:
                    dve.do(lambda e, n=n: e.tensor_copy(out_i[:, 0, 0:n], bank[0][:, 0:n]), store_free)
                    y_ = dve.do(lambda e, n=n, Y=Y: e.tensor_copy(Y, bank[1][:, 0:n]))
                    x_ = dve.do(lambda e, n=n, X=X, PLACE=PLACE: e.scalar_tensor_tensor(
                        out=X, in0=PLACE, scalar=float(REL), in1=bank[1][:, 0:n], op0=ALU.mult, op1=ALU.add), in_)
                    psum_free = dve.do(lambda e, n=n, Y=Y: e.scalar_tensor_tensor(
                        out=out_i[:, 1, 0:n], in0=bank[0][:, 0:n], scalar=float(REL), in1=Y, op0=ALU.mult,
                        op1=ALU.add), y_)
                    x_ = dve.do(lambda e, X=X, GE=GE, IN=IN: e.scalar_tensor_tensor(
                        out=GE, in0=X, scalar=1.0, in1=IN, op0=ALU.add, op1=ALU.mult), x_)
                    dve.do(lambda e, GE=GE, n=n: e.tensor_scalar(out_c[:, 0:n], GE, -1.0, None, ALU.add), x_)
                    g = dve.do(lambda e, WIN=WIN, n=n: e.tensor_copy(wrow_i[:, 0:n], WIN[0:1, :]))
                    sp.dma(scr_i[:, :, a0:a0 + n], out_i[:, :, 0:n], ch_s, g)
                    sp.dma(scr_c[:, a0:a0 + n], out_c[:, 0:n], ch_s)
                    store_free = sp.dma(scr_w[:, a0:a0 + n], wrow_i[:, 0:n], ch_s)
        t_plan = dve.last()
        cut = carved[0] * 2 // 3
        t_zero = [pool.do(lambda e: e.memset(flat[:, cut:carved[0]], 0.0), t_plan, store_free),
                  dve.do(lambda e: e.memset(flat[:, 0:cut], 0.0), t_plan, store_free, pe.last()), t_zero_rest]

        NL = 8
        NC = NB * WA * GA
        assert JA % GA == 0
        iota = sb("iota", [P, NC], F16, own)
        dist = sb("dist", [P, 4, P], F16, own)
        lo_hot = sb("lo_hot", [P, NL, P], F16, own)
        hi_hot = sb("hi_hot", [P, NL, NC], F16, own)
        t_iota = pool.do(lambda e: e.iota(iota[:, :], pattern=[[1, NC]], base=0, channel_multiplier=0,
                                          allow_small_or_imprecise_dtypes=True), t_plan, store_free)
        regs = {}
        mm_tok, lo_tok, hi_tok, add_tok, dist_tok = [], [], [], [], []

        def distance(j):
            if j < JA:
                dist_tok.append(act.do(lambda e: e.activation(dist[:, j % 4, :], iota[:, 0:P], ACT.Abs,
                                                              bias=nlo[:, j:j + 1], scale=1.0),
                                       t_iota, t_plan, lo_tok[j - 4] if j >= 4 else None))

        def hots(j):
            s = j % NL
            free = mm_tok[j - NL] if j >= NL else None
            lo_tok.append(act.do(lambda e: e.activation(lo_hot[:, s, :], dist[:, j % 4, :], ACT.Relu, bias=1.0,
                                                        scale=-1.0), dist_tok[j], free))
            distance(j + 2)
            hi_tok.append(dve.do(lambda e: e.tensor_scalar(hi_hot[:, s, :], iota[:, :], code[:, j:j + 1], None,
                                                           ALU.is_equal), t_iota, t_plan, free))

        distance(0)
        distance(1)
        for j in range(AHEAD):
            hots(j)
        for j in range(0, JA, GA):
            k = j // GA
            for q in range(GA):
                s = (j + q) % NL
                mm = pe.do(lambda e, s=s, k=k, q=q: e.matmul(bank[4 + k % 4][:, 0:NC], lo_hot[:, s, :], hi_hot[:, s, :],
                                                             start=(q == 0), stop=(q == GA - 1)),
                           lo_tok[j + q], hi_tok[j + q], add_tok[k - 4] if k >= 4 else None)
                mm_tok.append(mm)
            if j % (GA * REGS) == 0:
                n = min(REGS, (JA - j) // GA)

                def load(e, j=j, n=n):
                    if not regs:
                        regs["dve"] = [e.alloc_register(f"window{i}") for i in range(REGS)]
                    e.load(regs["dve"][0:n], wcol[0:1, j:j + GA * (n - 1) + 1:GA])
                dve.quiet(load)

            def add(e, k=k):
                c = e.snap(regs["dve"][k % REGS], min_val=0, max_val=NP - WA * GA)
                a = adj[:, :, bass.ds(c, WA * GA)]
                return e.tensor_tensor(a, a, bank[4 + k % 4][:, 0:NC].rearrange("p (h w) -> p h w", w=WA * GA), ALU.add)
            add_tok.append(dve.do(add, mm, add_tok[k - 1] if k else None, *t_zero))
            for q in range(GA):
                if j + q + AHEAD < JA:
                    hots(j + q + AHEAD)
        own.close()
        for b in range(NB):
            t_self = dve.do(lambda e, b=b: e.tensor_tensor(adj[:, b, b * P:b * P + P], adj[:, b, b * P:b * P + P],
                                                           ident16[:, :], ALU.add), add_tok[-1], t_ident)
        adj_ready = t_self

        dense = ExitStack()
        split = sb("split", [P, NB, 2, D], F16, dense)
        hT = split[:, :, :, :].rearrange("p b s d -> p (b s d)").bitcast(F32)
        weights = sb("weights", [P, 7, D], F32, dense)
        deg = sb("deg", [P, NB], F32, dense)
        dinv = sb("dinv", [P, NB], F32, dense)
        ch_w = channel("ch_weights")
        WT = {}
        for k, name in enumerate(["L0_gnn_W1", "L0_gnn_W2", "L0_gnn_W3", "L1_gnn_W", "L2_gnn_W1", "L2_gnn_W2"]):
            WT[name] = weights[:, k, :]
            t_w = sp.dma(weights[:, k, :], io[name], ch_w, t_self)

        def turn(ready, solo=0):
            token = ready
            k = 0
            freed = [None] * 8
            ends_ = []
            pairs = []
            for i in range(NB):
                pairs.append((i, i, 1))
                for j0 in range(i + 1, NB, 8):
                    pairs.append((i, j0, min(8, NB - j0)))
            for i, j0, n in pairs:
                pa, pb = (2 * k) % 8, (2 * k + 1) % 8
                k += 1
                va = bank[pa][:, :].bitcast(F16)
                vb = bank[pb][:, :].bitcast(F16)
                pe.wait(token, t_ident, freed[pa], freed[pb])
                for m in range(n):
                    j = j0 + m
                    f = lambda e, m=m, j=j, i=i, va=va: e.transpose(va[:, m * P:m * P + P], adj[:, i, j * P:j * P + P], ident16[:, :])
                    if m == n - 1:
                        w1 = pe.do(f)
                    else:
                        pe.quiet(f)
                w2 = w1
                if j0 != i:
                    for m in range(n):
                        j = j0 + m
                        f = lambda e, m=m, j=j, i=i, vb=vb: e.transpose(vb[:, m * P:m * P + P], adj[:, j, i * P:i * P + P], ident16[:, :])
                        if m == n - 1:
                            w2 = pe.do(f)
                        else:
                            pe.quiet(f)
                freed[pa] = act.do(lambda e, i=i, j0=j0, n=n, va=va: e.activation(
                    adj[:, j0:j0 + n, i * P:i * P + P], va[:, 0:n * P].rearrange("p (n q) -> p n q", q=P), ACT.Copy), w2)
                ends_.append(freed[pa])
                if j0 != i:
                    if k <= solo:
                        freed[pb] = act.do(lambda e, i=i, j0=j0, n=n, vb=vb: e.activation(
                            adj[:, i, j0 * P:(j0 + n) * P], vb[:, 0:n * P], ACT.Copy), w2)
                    else:
                        freed[pb] = dve.do(lambda e, i=i, j0=j0, n=n, vb=vb: e.tensor_copy(
                            adj[:, i, j0 * P:(j0 + n) * P], vb[:, 0:n * P]), w2)
                    ends_.append(freed[pb])
            return [act.last(), dve.last()]

        def degrees(ready, to):
            pe.wait(*ready, t_const)
            for b in range(NB):
                for k in range(NB):
                    f = lambda e, b=b, k=k: e.matmul(bank[7][:, b:b + 1], adj[:, k, b * P:b * P + P], ones16[:, :],
                                                     start=(k == 0), stop=(k == NB - 1))
                    if b == NB - 1 and k == NB - 1:
                        w = pe.do(f)
                    else:
                        pe.quiet(f)
            return dve.do(lambda e: e.tensor_copy(to[:, :], bank[7][:, 0:NB]), w)

        def aggregate(ready, block_ready, unscale, eps_rhs=None):
            pe.wait(*ready)
            for k in range(NB):
                pe.wait(*block_ready[k])
                for s in range(2):
                    for c, (c0, n) in enumerate(chunk):
                        last = k == NB - 1 and s == 1
                        f = lambda e, k=k, s=s, c=c, c0=c0, n=n, last=last: e.matmul(
                            bank[c][:, 0:n], split[:, k, s, :], adj[:, k, c0:c0 + n],
                            start=(k == 0 and s == 0), stop=last)
                        if last and c == NCH - 1:
                            w = pe.do(f)
                        else:
                            pe.quiet(f)
                    if eps_rhs is not None and k == NB - 1 and s == 0:
                        for b in range(NB):
                            pe.quiet(lambda e, b=b: e.matmul(
                                bank[b * P // CH][:, b * P % CH:b * P % CH + P], xres[:, b, :], eps_rhs,
                                start=False, stop=False, skip_group_check=True))
            toks = []
            for c, (c0, n) in enumerate(chunk):
                if c % 2:
                    toks.append(dve.do(lambda e, c=c, c0=c0, n=n: e.tensor_scalar(zT[:, c0:c0 + n], bank[c][:, 0:n],
                                                                                 unscale, None, ALU.mult), w))
                else:
                    toks.append(act.do(lambda e, c=c, c0=c0, n=n: e.activation(zT[:, c0:c0 + n], bank[c][:, 0:n],
                                                                               ACT.Copy if isinstance(unscale, float) else ACT.Identity,
                                                                               scale=unscale), w))
            return toks

        def project(ready, W, fold):
            pe.wait(*ready)
            for i, quad in enumerate(quads):
                for b in quad:
                    w = pe.do(lambda e, b=b, i=i: e.matmul(bank[i][:, b % 4 * P:b % 4 * P + P], zT[:, b * P:b * P + P], W,
                                                           start=True, stop=True))
                folded = {b: fold(b, bank[i][:, b % 4 * P:b % 4 * P + P], w) for b in quad}
                t = stats_of(znode, quad, folded)
            return t

        def rsqrt(to, var, eps, ready):
            n = to.shape[1]
            v, r = root[:, 0, 0:n], root[:, 1, 0:n]
            a = dve.do(lambda e: e.tensor_scalar(v, var, eps, None, ALU.add), ready)
            a = act.do(lambda e: e.activation(r, v, ACT.Sqrt), a)
            a = dve.do(lambda e: e.reciprocal(to, r), a)
            a = dve.do(lambda e: e.tensor_tensor(r, to, to, ALU.mult), a)
            a = dve.do(lambda e: e.tensor_tensor(r, r, v, ALU.mult), a)
            a = dve.do(lambda e: e.tensor_scalar(r, r, -0.5, 1.5, ALU.mult, ALU.add), a)
            return dve.do(lambda e: e.tensor_tensor(to, to, r, ALU.mult), a)

        quads = [range(b, min(b + 4, NB)) for b in range(0, NB, 4)]

        def stats_of(src, quad, ready):
            for b in quad:
                a = dve.do(lambda e, b=b: e.bn_stats(stats[:, b, :], src[:, b, :]), ready[b])
            for b in quad:
                c = dve.do(lambda e, b=b: e.bn_aggr(mv[:, b, :], stats[:, b, :]), a)
            return c

        def norm_params(ready):
            d = rsqrt(rstd[:, :], mv[:, :, 1], EPS, ready)
            return dve.do(lambda e: e.scalar_tensor_tensor(out=nmr[:, :], in0=mv[:, :, 0], scalar=-1.0, in1=rstd[:, :],
                                                           op0=ALU.mult, op1=ALU.mult), d)

        def normalize(dst, src, quad, ready, both=True):
            last = {}
            for b in quad:
                if b % 2 and both:
                    last[1] = act.do(lambda e, b=b: e.activation(dst[:, b, :], src[:, b, :], ACT.Identity,
                                                                 bias=nmr[:, b:b + 1], scale=rstd[:, b:b + 1]), ready)
                else:
                    last[0] = dve.do(lambda e, b=b: e.tensor_scalar(dst[:, b, :], src[:, b, :], rstd[:, b:b + 1],
                                                                    nmr[:, b:b + 1], ALU.mult, ALU.add), ready)
            return list(last.values())

        def norm_all(dst, src, ready, both=True):
            for quad in quads:
                t = stats_of(src, quad, ready)
            t = norm_params(t)
            done_ = {}
            for quad in quads:
                n = normalize(dst, src, quad, t, both)
                for b in quad:
                    done_[b] = n
            return done_

        def bcast(row, n=NB):
            return row.unsqueeze(1).broadcast_to([P, n, D])

        def percol(col):
            return col.unsqueeze(2).broadcast_to([P, col.shape[1], D])

        def split_parts(src, quad, scale, ready):
            q0, q1 = quad[0], quad[-1] + 1
            hi = act.do(lambda e: e.activation(split[:, q0:q1, 0, :], src[:, q0:q1, :],
                                               ACT.Copy if isinstance(scale, float) else ACT.Identity, scale=scale), *ready)
            lo = dve.do(lambda e: e.scalar_tensor_tensor(out=split[:, q0:q1, 1, :], in0=src[:, q0:q1, :], scalar=scale,
                                                         in1=split[:, q0:q1, 0, :], op0=ALU.mult, op1=ALU.subtract), hi)
            return [hi, lo]

        turned = turn(adj_ready)
        t_deg = degrees(turned, deg)
        t_dinv = rsqrt(dinv[:, :], deg[:, :], 0.0, t_deg)

        def power_scale(k, top, ready):
            d = dve.do(lambda e: e.tensor_scalar(small[:, k:k + 1], top, 2.0 ** -100, 2.0 ** 110, ALU.max, ALU.min), ready)
            d = dve.do(lambda e: e.tensor_scalar(smalli[:, 0:1], small[:, k:k + 1].bitcast(I32), 0x7F800000, None,
                                                 ALU.bitwise_and), d)
            d = dve.do(lambda e: e.tensor_scalar(small[:, k + 1:k + 2], smalli[:, 0:1].bitcast(F32), 2.0 ** -14, None,
                                                 ALU.mult), d)
            return dve.do(lambda e: e.reciprocal(small[:, k:k + 1], small[:, k + 1:k + 2]), d)

        b_ = dve.do(lambda e: e.tensor_reduce(small[:, 6:7], xres[:, :, :].rearrange("p b d -> p (b d)"), AX.X, ALU.max,
                                              apply_absolute_value=True), t_x)
        b_ = pool.do(lambda e: e.partition_all_reduce(small[:, 7:8], small[:, 6:7], P, bass.bass_isa.ReduceOp.max), b_)
        scaled_ready = {1: power_scale(0, small[:, 7:8], b_)}
        for layer in (1, 2):
            for q, name in enumerate((f"L0_gnn_g{layer}", f"L0_gnn_beta{layer}")):
                b_ = dve.do(lambda e, q=q, name=name: e.tensor_reduce(small[:, 8 + q:9 + q], ROW[name], AX.X, ALU.max,
                                                                      apply_absolute_value=True), dve.last(), t_param)
            b_ = dve.do(lambda e: e.scalar_tensor_tensor(out=small[:, 10:11], in0=small[:, 8:9], scalar=float(D) ** 0.5,
                                                         in1=small[:, 9:10], op0=ALU.mult, op1=ALU.add), b_)
            scaled_ready[layer + 1] = power_scale(2 * layer, small[:, 10:11], b_)

        block_ready = {}
        for quad in quads:
            q0, q1 = quad[0], quad[-1] + 1
            a = dve.do(lambda e, q0=q0, q1=q1: e.tensor_tensor(znode[:, q0:q1, :], xres[:, q0:q1, :],
                                                               percol(dinv[:, q0:q1]), ALU.mult), t_dinv)
            t = split_parts(znode, quad, small[:, 0:1], [a, *scaled_ready.values()])
            block_ready.update({b: t for b in quad})
        for layer in (1, 2, 3):
            W, bias = WT[f"L0_gnn_W{layer}"], ROW[f"L0_gnn_b{layer}"]
            gain, beta = ROW[f"L0_gnn_g{layer}"], ROW[f"L0_gnn_beta{layer}"]
            z = aggregate(turned, block_ready, small[:, 2 * layer - 1:2 * layer])

            def fold(b, ps, w, bias=bias):
                return dve.do(lambda e: e.scalar_tensor_tensor(out=znode[:, b, :], in0=ps, scalar=dinv[:, b:b + 1],
                                                               in1=bias, op0=ALU.mult, op1=ALU.add), w)
            t = project([*z, t_w], W, fold)
            p = norm_params(t)
            block_ready, summed = {}, {}
            for quad in quads:
                q0, q1 = quad[0], quad[-1] + 1
                zq, n = znode[:, q0:q1, :], q1 - q0
                a = normalize(znode, znode, quad, p, layer < 3)
                a = dve.do(lambda e, g=gain, zq=zq, n=n: e.tensor_tensor(zq, zq, bcast(g, n), ALU.mult), *a)
                a = dve.do(lambda e, g=beta, zq=zq, n=n: e.tensor_tensor(zq, zq, bcast(g, n), ALU.add), a)
                if layer < 3:
                    a = dve.do(lambda e, zq=zq, q0=q0, q1=q1: e.scalar_tensor_tensor(
                        out=zq, in0=zq, scalar=0.0, in1=percol(dinv[:, q0:q1]), op0=ALU.max, op1=ALU.mult), a)
                    s_ = split_parts(znode, quad, small[:, 2 * layer:2 * layer + 1], [a])
                    block_ready.update({b: s_ for b in quad})
                else:
                    a = dve.do(lambda e, zq=zq, q0=q0, q1=q1: e.scalar_tensor_tensor(
                        out=zq, in0=zq, scalar=0.0, in1=xres[:, q0:q1, :], op0=ALU.max, op1=ALU.add), a)
                    t = stats_of(znode, quad, {b: a for b in quad})
        l0_projected = p

        def next_stream(t, scale=FX):
            p = norm_params(t)
            ready, xr_ = {}, {}
            for quad in quads:
                n = normalize(xres, znode, quad, p)
                xr_.update({b: n for b in quad})
                s_ = split_parts(xres, quad, scale, n)
                ready.update({b: s_ for b in quad})
            return xr_, ready
        back = turn(l0_projected, solo=18)
        x_blocks, block_ready = next_stream(t)
        t_cnt = degrees(back, deg)
        z = aggregate(back, block_ready, 1.0 / FX)
        tr = pe.do(lambda e: e.transpose(bank[7][:, 0:P], WT["L1_gnn_W"], ident[:, :]), t_cnt)
        tr = dve.do(lambda e: e.tensor_copy(weights[:, 6, :], bank[7][:, 0:P]), tr)

        def fold1(b, ps, w):
            a = dve.do(lambda e: e.scalar_tensor_tensor(out=znode[:, b, :], in0=ROW["L1_gnn_b"], scalar=deg[:, b:b + 1],
                                                        in1=ps, op0=ALU.mult, op1=ALU.add), w, t_cnt)
            return dve.do(lambda e: e.tensor_tensor(znode[:, b, :], znode[:, b, :], xres[:, b, :], ALU.add), a, *x_blocks[b])
        t = project([*z, tr], weights[:, 6, :], fold1)
        t_eps_free = pe.last()

        eps_id = weights[:, 6, :]
        ei = dve.do(lambda e: e.tensor_scalar(eps_id, ident[:, :], colp[:, 10:11], FX, ALU.mult, ALU.mult), t_eps_free, t_param)
        x_blocks, block_ready = next_stream(t)
        z = aggregate([ei], block_ready, 1.0 / FX, eps_id)
        adj_free = pe.last()
        cur, nxt = zT[:, :], hT
        ready = z
        bstat = stats[:, 0:NCH, :]
        for layer in (1, 2):
            W = WT[f"L2_gnn_W{layer}"]
            b_, g_, be_ = (COL[f"L2_gnn_{n}{layer}"] for n in ("b", "g", "beta"))
            pe.wait(*ready)
            toks = []
            for c, (c0, n) in enumerate(chunk):
                w = pe.do(lambda e, c=c, c0=c0, n=n, cur=cur, W=W: e.matmul(bank[c][:, 0:n], W, cur[:, c0:c0 + n],
                                                                           start=True, stop=True))
                a = act.do(lambda e, c=c, c0=c0, n=n, nxt=nxt, b_=b_: e.activation(nxt[:, c0:c0 + n], bank[c][:, 0:n],
                                                                                   ACT.Identity, bias=b_, scale=1.0), w, t_param)
                m = min(n, N - c0)
                a = dve.do(lambda e, c=c, c0=c0, m=m, nxt=nxt: e.bn_stats(bstat[:, c, :], nxt[:, c0:c0 + m]), a)
            a = dve.do(lambda e: e.bn_aggr(mv[:, 0, :], bstat), a)
            a = rsqrt(small[:, 5:6], mv[:, 0, 1:2], EPS, a)
            a = dve.do(lambda e, g_=g_: e.tensor_tensor(small[:, 6:7], small[:, 5:6], g_, ALU.mult), a)
            a = dve.do(lambda e: e.tensor_tensor(small[:, 7:8], mv[:, 0, 0:1], small[:, 6:7], ALU.mult), a)
            a = dve.do(lambda e, be_=be_: e.tensor_tensor(small[:, 8:9], be_, small[:, 7:8], ALU.subtract), a)
            half = 4 * CH
            r1 = act.do(lambda e, nxt=nxt: e.activation(nxt[:, 0:half], nxt[:, 0:half], ACT.Relu, bias=small[:, 8:9],
                                                        scale=small[:, 6:7]), a)
            r2 = act.do(lambda e, nxt=nxt: e.activation(nxt[:, half:NP], nxt[:, half:NP], ACT.Relu, bias=small[:, 8:9],
                                                        scale=small[:, 6:7]), a)
            cur, nxt = nxt, cur
            ready = [r1, r2]
        toks = []
        for b in range(NB):
            c, o = b // 4 % 7, b % 4 * P
            w = pe.do(lambda e, b=b, c=c, o=o, cur=cur: e.transpose(bank[c][:, o:o + P], cur[:, b * P:b * P + P], ident[:, :]),
                      *ready)
            if b % 4 == 3 or b == NB - 1:
                b0 = b // 4 * 4
                n = b + 1 - b0
                toks = dve.do(lambda e, b0=b0, n=n: e.tensor_tensor(
                    xres[:, b0:b0 + n, :], xres[:, b0:b0 + n, :],
                    bank[b0 // 4 % 7][:, 0:n * P].rearrange("p (b d) -> p b d", d=P), ALU.add), w)
        x_blocks = norm_all(xres, xres, {b: toks for b in range(NB)})
        x_ready = [t for ts in x_blocks.values() for t in ts]
        dense.close()
        adj_ctx.close()

        rel = ExitStack()
        sums = sb("sums", [P, NW4, G, D + 1], F32, rel)
        NG = 6
        gath = sb("gath", [P, NG, 3 * D + 1], BF16, rel)
        hot = sb("hot", [P, NG, G * P], BF16, rel)
        iota_r = sb("iota_r", [P, G * P], F16, rel)
        index = sb("index", [P, 2, JR], I32, rel)
        code_r = sb("code_r", [P, JR], F32, rel)
        win = sb("win", [1, JR], I32, rel)
        place = sb("place", [P, REL, P], F32, rel)
        inv = sb("inv", [P, NW4 * G], F32, rel)
        w1 = sb("w1", [P, REL, H], F32, rel)
        root1 = sb("root1", [P, H], F32, rel)
        w2 = sb("w2", [P, HB, REL, D], F32, rel)
        root2 = sb("root2", [P, HB, D], F32, rel)
        parts = sb("parts", [P, 2, REL, 3, D], BF16, rel)
        rest = sb("rest", [P, REL * D], F32, rel)
        relT = sb("relT", [P, 2, REL, P], F32, rel)
        hTr = sb("hTr", [P, 2, HB, P], F32, rel)
        xT = sb("xT", [P, 2, P], F32, rel)
        free_mem = [adj_free, dve.last(), act.last(), pe.last()]

        ch_l3, ch_l4 = channel("ch_l3"), channel("ch_l4")
        sp.wait(*free_mem, store_free)
        sp.dma(index[:, :, :], scr_i, ch_l3)
        sp.dma(code_r[:, :], scr_c, ch_l3)
        t_lists = sp.dma(win[:, :], scr_w, ch_l3)
        sp.dma(w1[:, :, :], io["L3_gnn_W1"].rearrange("r k o -> k r o"), ch_l4)
        sp.dma(root1[:, :], io["L3_gnn_root1"], ch_l4)
        for h in range(HB):
            sp.dma(w2[:, h, :, :], io["L3_gnn_W2"][:, h * P:h * P + P, :].rearrange("r k o -> k r o"), ch_l4)
        t_w3 = sp.dma(root2[:, :, :], io["L3_gnn_root2"].rearrange("(h k) o -> k h o", k=P), ch_l4)

        pool.wait(*free_mem)
        z0 = pool.do(lambda e: e.memset(gath[:, :, :], 1.0))
        z0 = pool.do(lambda e: e.iota(iota_r[:, :], pattern=[[1, G * P]], base=0, channel_multiplier=0,
                                      allow_small_or_imprecise_dtypes=True))
        z1 = pool.do(lambda e: e.memset(place[:, :, :], 1.0))
        z1 = pool.do(lambda e: e.affine_select(out=place[:, :, :], in_=place[:, :, :], compare_op=ALU.is_ge, fill=0.0,
                                               base=0, pattern=[[REL * GN, P // GN], [-REL, P]], channel_multiplier=1), z1)
        t_place = pool.do(lambda e: e.affine_select(out=place[:, :, :], in_=place[:, :, :], compare_op=ALU.is_ge, fill=0.0,
                                                    base=REL - 1, pattern=[[-REL * GN, P // GN], [REL, P]],
                                                    channel_multiplier=-1), z1)
        half_w = NW4 // 2
        z2 = pool.do(lambda e: e.memset(sums[:, half_w:NW4, :, :], 0.0))
        z3 = dve.do(lambda e: e.memset(sums[:, 0:half_w, :, :], 0.0), *free_mem)
        sums_zero = [z2, z3]

        def three_parts(dst3, src, scratch, ready, n):
            a = act.do(lambda e: e.activation(dst3(0), src, ACT.Copy), *ready)
            a = dve.do(lambda e: e.tensor_tensor(scratch, src, dst3(0), ALU.subtract), a)
            b = act.do(lambda e: e.activation(dst3(1), scratch, ACT.Copy), a)
            b = dve.do(lambda e: e.tensor_tensor(dst3(2), scratch, dst3(1), ALU.subtract), b)
            return b

        ch_t1 = channel("ch_table1")
        part_free = [None, None]
        NBH = REL
        for i, b0 in enumerate(range(0, NB, NBH)):
            n = min(NBH, NB - b0)
            s = i % 2
            scratch = rest[:, 0:n * D].rearrange("p (b d) -> p b d", d=D)
            t = three_parts(lambda q, s=s, n=n: parts[:, s, 0:n, q, :], xres[:, b0:b0 + n, :], scratch,
                            [*x_ready, *free_mem, part_free[s]], n)
            part_free[s] = sp.dma(table1[b0 * P:(b0 + n) * P, :].rearrange("(b p) f -> p b f", p=P),
                                  parts[:, s, 0:n, :, :].rearrange("p b q d -> p b (q d)"), ch_t1, t)
            dve.wait(part_free[s])
        t_table1 = part_free[(len(range(0, NB, NBH)) - 1) % 2]

        ch_g = [channel(f"ch_gather{i}") for i in range(NG)]
        dregs = {"r": None}

        def relation_sums(table, which, ready):
            gt, ht, mt, at = [], [], [], []
            pool.wait(*ready, t_lists, z0)
            dve.wait(*sums_zero, t_lists, z0)

            def gather(j):
                s = j % NG
                ch = ch_g[s]
                ch[1] += 16
                pool.wait(mt[j - NG] if j >= NG else None)
                pool.program.append(lambda e, s=s, j=j: e.indirect_dma_start(
                    gath[:, s, 0:3 * D], None, table,
                    bass.IndirectOffsetOnAxis(ap=index[:, which, j:j + 1].bitcast(U32), axis=0)).then_inc(ch_g[s][0], 16))
                gt.append((ch[0], ch[1]))

            def one_hot(j):
                s = j % NG
                ht.append(dve.do(lambda e, s=s, j=j: e.tensor_scalar(hot[:, s, :], iota_r[:, :], code_r[:, j:j + 1], None,
                                                                     ALU.is_equal), mt[j - NG] if j >= NG else None))

            for j in range(AHEAD):
                one_hot(j)
            for j in range(JR):
                s = j % NG
                gather(j)
                pe.wait(gt[j], ht[j], at[j - 4] if j >= 4 else None)
                ps = bank[j % 4]
                for g in range(G):
                    for q, (a, b) in enumerate([(2 * D, 3 * D + 1), (D, 2 * D), (0, D)]):
                        f = lambda e, g=g, q=q, a=a, b=b, s=s, ps=ps: e.matmul(
                            ps[:, g * (D + 1):g * (D + 1) + b - a], hot[:, s, g * P:g * P + P], gath[:, s, a:b],
                            start=(q == 0), stop=(q == 2), skip_group_check=True)
                        if g == G - 1 and q == 2:
                            m = pe.do(f)
                        else:
                            pe.quiet(f)
                mt.append(m)
                if j % REGS == 0:
                    n = min(REGS, JR - j)

                    def load(e, j=j, n=n):
                        dregs["r"] = regs["dve"]
                        e.load(dregs["r"][0:n], win[0:1, j:j + n])
                    dve.quiet(load)

                def add(e, j=j, ps=ps):
                    c = e.snap(dregs["r"][j % REGS], min_val=0, max_val=NW4 - 1)
                    a = sums[:, bass.ds(c, 1), :, :].rearrange("p o g d -> p (o g d)")
                    return e.tensor_tensor(a, a, ps[:, 0:G * (D + 1)], ALU.add)
                if j:
                    prev = at[j - 1]
                else:
                    prev = None
                at.append(dve.do(add, mt[j], prev))
                if j + AHEAD < JR:
                    one_hot(j + AHEAD)
            cnt = sums[:, :, :, D].rearrange("p w g -> p (w g)")
            a = dve.do(lambda e: e.tensor_scalar(inv[:, :], cnt, 1.0, None, ALU.max), at[-1])
            return dve.do(lambda e: e.reciprocal(inv[:, :], inv[:, :]), a)

        GB = WPB * G
        sums_g = sums[:, :, :, :].rearrange("p w g d -> p (w g) d")

        done = relation_sums(table1, 0, [t_table1])
        root_out = znode
        ch_t2 = [channel(f"ch_table2_{i}") for i in range(2)]
        relT_free, hT_free = [None, None], [None, None]
        b7 = None
        bank_free = [None] * 8
        zero_tok = None
        pe.wait(t_w3)
        part_free = [part_free[0], part_free[1]]
        scaled, relT_done, hT_done = {}, {}, {}

        def scale_rows(nb):
            g0 = nb * GB
            scaled[nb] = dve.do(lambda e: e.tensor_tensor(
                sums_g[:, g0:g0 + GB, 0:D], sums_g[:, g0:g0 + GB, 0:D],
                inv[:, g0:g0 + GB].unsqueeze(2).broadcast_to([P, GB, D]), ALU.mult), done)

        def turn_rows(nb):
            s, g0 = nb % 2, nb * GB
            for h in range(2):
                pe.wait(scaled[nb], bank_free[h])
                for q in range(4):
                    m = pe.do(lambda e, h=h, q=q: e.transpose(bank[h][:, q * P:q * P + P],
                                                              sums_g[:, g0 + 4 * h + q, 0:D], ident[:, :]))
                bank_free[h] = act.do(lambda e, h=h: e.activation(
                    relT[:, s, :, h * 4 * GN:(h + 1) * 4 * GN].rearrange("p r n -> p n r"),
                    bank[h][:, :].rearrange("p (n r) -> p n r", r=REL), ACT.Copy), m, relT_free[s])
            zeroed.append(pool.do(lambda e: e.memset(sums_g[:, g0:g0 + GB, :], 0.0), m, done))
            m = pe.do(lambda e: e.transpose(bank[2][:, 0:P], xres[:, nb, :], ident[:, :]), bank_free[2], *x_ready)
            bank_free[2] = act.do(lambda e: e.activation(xT[:, s, :], bank[2][:, 0:P], ACT.Copy), m, relT_free[s])
            relT_done[nb] = [bank_free[0], bank_free[1], bank_free[2]]

        def hidden(nb):
            s = nb % 2
            pe.wait(*relT_done[nb], bank_free[3])
            for o in range(HB):
                for r in range(REL):
                    pe.quiet(lambda e, o=o, r=r: e.matmul(bank[3][:, o * P:o * P + P], w1[:, r, o * P:o * P + P],
                                                          relT[:, s, r, :], start=(r == 0), stop=False,
                                                          skip_group_check=True))
                m = pe.do(lambda e, o=o: e.matmul(bank[3][:, o * P:o * P + P], root1[:, o * P:o * P + P],
                                                  xT[:, s, :], start=False, stop=True, skip_group_check=True))
            relT_free[s] = m
            for o in range(HB):
                hT_done[nb] = bank_free[3] = act.do(lambda e, o=o: e.activation(
                    hTr[:, s, o, :], bank[3][:, o * P:o * P + P], ACT.Relu, bias=colp[:, 8 + o:9 + o], scale=1.0),
                    m, hT_free[s])

        def table_rows(nb):
            s = nb % 2
            m = None
            for y in range(2):
                pe.wait(hT_done[nb], bank_free[4 + y])
                for k in range(HB):
                    m = pe.do(lambda e, y=y, k=k: e.matmul(
                        bank[4 + y][:, :], hTr[:, s, k, :], w2[:, k, 4 * y:4 * y + 4, :].rearrange("p r d -> p (r d)"),
                        start=(k == 0), stop=(k == HB - 1)))
                scratch = rest[:, y * CH:(y + 1) * CH].rearrange("p (r d) -> p r d", d=D)
                bank_free[4 + y] = three_parts(lambda q, y=y: parts[:, s, 4 * y:4 * y + 4, q, :],
                                               bank[4 + y][:, :].rearrange("p (r d) -> p r d", d=D), scratch,
                                               [m, part_free[s]], 4)
            pe.wait(bank_free[6])
            for k in range(HB):
                m = pe.do(lambda e, k=k: e.matmul(bank[6][:, 0:P], hTr[:, s, k, :], root2[:, k, :],
                                                  start=(k == 0), stop=(k == HB - 1)))
            hT_free[s] = m
            bank_free[6] = dve.do(lambda e: e.tensor_tensor(root_out[:, nb, :], bank[6][:, 0:P], ROW["L3_gnn_b2"],
                                                            ALU.add), m, *x_ready)
            part_free[s] = sp.dma(table2[nb * P * REL:(nb + 1) * P * REL, :].rearrange("(p r) f -> p (r f)", r=REL),
                                  parts[:, s, :, :, :].rearrange("p r q d -> p (r q d)"), ch_t2[s], bank_free[4], bank_free[5])

        zeroed = []
        scale_rows(0)
        scale_rows(1)
        turn_rows(0)
        for nb in range(NB):
            hidden(nb)
            if nb + 1 < NB:
                turn_rows(nb + 1)
            if nb + 2 < NB:
                scale_rows(nb + 2)
            table_rows(nb)
        zero_tok = zeroed[-1]
        xr = dve.do(lambda e: e.tensor_tensor(root_out, root_out, xres[:, :, :], ALU.add), dve.last())
        t_table2 = part_free[(NB - 1) % 2]

        sums_zero = [zero_tok]
        done = relation_sums(table2, 1, [t_table2, part_free[0], part_free[1]])
        bf = [None] * 8
        for nb in range(NB):
            g0 = nb * GB
            c = nb % 4
            a = dve.do(lambda e, g0=g0: e.tensor_tensor(
                sums_g[:, g0:g0 + GB, 0:D], sums_g[:, g0:g0 + GB, 0:D],
                inv[:, g0:g0 + GB].unsqueeze(2).broadcast_to([P, GB, D]), ALU.mult), done)
            pe.wait(a, bf[c], t_place)
            for q in range(GB):
                f = lambda e, q=q, g0=g0, c=c: e.matmul(bank[c][:, 0:D], place[:, q, :], sums_g[:, g0 + q, 0:D],
                                                        start=(q == 0), stop=(q == GB - 1))
                m = pe.do(f)
            bf[c] = dve.do(lambda e, nb=nb, c=c: e.tensor_tensor(root_out[:, nb, :], root_out[:, nb, :], bank[c][:, 0:D],
                                                                 ALU.add), m, xr)
        final = [t for ts in norm_all(xres, znode, {b: dve.last() for b in range(NB)}).values() for t in ts]
        ch_o = channel("ch_out")
        sp.dma(out[0:FULL * P, :].rearrange("(b p) d -> p b d", p=P), xres[:, 0:FULL, :], ch_o, *final)
        t_out = sp.dma(out[FULL * P:N, :], xres[0:TAILN, FULL, :], ch_o)
        sp.wait(t_out)
        rel.close()

        block = ctx.enter_context(nc.Block())

        @block.tensor
        def _(e):
            pe.replay(e)

        @block.vector
        def _(e):
            dve.replay(e)

        @block.scalar
        def _(e):
            act.replay(e)

        @block.gpsimd
        def _(e):
            pool.replay(e)

        @block.sync
        def _(e):
            sp.replay(e)


_INS = ['x', 'src', 'dst', 'edge_type_8'] + [f"L0_gnn_{p}{i}" for i in (1, 2, 3) for p in ("W", "b", "g", "beta")] + \
    ['L1_gnn_W', 'L1_gnn_b', 'L2_gnn_eps', 'L2_gnn_W1', 'L2_gnn_b1', 'L2_gnn_g1', 'L2_gnn_beta1', 'L2_gnn_W2',
     'L2_gnn_b2', 'L2_gnn_g2', 'L2_gnn_beta2', 'L3_gnn_W1', 'L3_gnn_root1', 'L3_gnn_b1', 'L3_gnn_W2',
     'L3_gnn_root2', 'L3_gnn_b2']


def kernel(**inputs):
    import numpy as _np
    import concourse.bacc as _bacc
    from concourse import mybir as _mybir
    from concourse.bass_utils import run_bass_kernel_spmd as _run

    nc = _bacc.Bacc("TRN2", target_bir_lowering=False, num_devices=1)
    arrays, io = {}, {}
    for name in _INS:
        a = _np.ascontiguousarray(inputs[name])
        arrays[f"in_{name}_dram"] = a
        io[name] = nc.dram_tensor(f"in_{name}_dram", a.shape, _mybir.dt.from_np(a.dtype), kind="ExternalInput").ap()
    x = arrays["in_x_dram"]
    out = nc.dram_tensor("out_0_dram", x.shape, _mybir.dt.from_np(x.dtype), kind="ExternalOutput").ap()
    gnn_stack(nc, io, out)
    r = _run(nc, [arrays], core_ids=[0])
    return r.results[0]["out_0_dram"]
```

```python
from contextlib import ExitStack

import concourse.bass as bass
from concourse import mybir

ALU = mybir.AluOpType
ACT = mybir.ActivationFunctionType
AX = mybir.AxisListType
F32 = mybir.dt.float32
F16 = mybir.dt.float16
I32 = mybir.dt.int32
U32 = mybir.dt.uint32

P = 128
EPS = 1e-5
REL = 8
WA = 8
WA_LOG2 = 3
GA = 2
WR = 64
WR_LOG2 = 6
REGS = 32
ACT_SHARE = (4, 9)
AHEAD = 4


class Lane:

    def __init__(self, sem):
        self.sem, self.count, self.program, self.seen = sem, 0, [], {}

    def wait(self, *tokens):
        for token in tokens:
            if token is None:
                continue
            sem, value = token
            if self.seen.get(id(sem), 0) < value:
                self.seen[id(sem)] = value
                self.program.append(lambda e, s=sem, v=value: e.wait_ge(s, v))

    def do(self, emit, *tokens):
        self.wait(*tokens)
        self.count += 1
        self.program.append(lambda e, f=emit, s=self.sem: f(e).then_inc(s, 1))
        return (self.sem, self.count)

    def quiet(self, emit, *tokens):
        self.wait(*tokens)
        self.program.append(lambda e, f=emit: f(e))

    def dma(self, out, in_, channel, *tokens, **how):
        self.wait(*tokens)
        channel[1] += 16
        self.program.append(lambda e, s=channel[0]: e.dma_start(out, in_, **how).then_inc(s, 16))
        return (channel[0], channel[1])

    def last(self):
        return (self.sem, self.count) if self.count else None

    def replay(self, e):
        for step in self.program:
            step(e)


def gnn_stack(nc, io, out):
    N, D = io["x"].shape
    E = io["src"].shape[0]
    NB = -(-N // P)
    NP = NB * P
    FULL = N // P
    TAILN = N - FULL * P
    T = -(-E // P)
    TB = -(-T // P)
    TFULL = (E // P) // P
    TROWS = E // P - TFULL * P
    TREST = E - (E // P) * P
    TLAST = T - TFULL * P
    JA = T + -(-N // WA) - 1
    JR = T + -(-N // WR) - 1
    H = io["L3_gnn_W1"].shape[2]
    HB = H // P
    CH = 512
    NCH = -(-NP // CH)
    chunk = [(c * CH, min(CH, NP - c * CH)) for c in range(NCH)]
    G = WR * REL // P
    GN = P // REL
    NW4 = NB * P // WR
    WPB = P // WR
    FX = 1024.0

    ctx = ExitStack()
    with ctx:
        def sem(name):
            return ctx.enter_context(nc.semaphore(name))

        def channel(name):
            return [sem(name), 0]

        def sb(name, shape, dt, where=None):
            return (where or ctx).enter_context(nc.sbuf_tensor(name, shape, dt))

        pe, dve, act, pool, sp = (Lane(sem(f"s_{n}")) for n in ("pe", "dve", "act", "pool", "sp"))
        pair = [ctx.enter_context(nc.psum_tensor(f"banks{i}", [P, 2 * CH], F32)) for i in range(4)]
        bank = [pair[i // 2][:, i % 2 * CH:(i % 2 + 1) * CH] for i in range(8)]

        ident = sb("ident", [P, P], F32)
        ident16 = sb("ident16", [P, P], F16)
        ones16 = sb("ones16", [P, 1], F16)
        ones_row = sb("ones_row", [1, P], F32)
        xres = sb("xres", [P, NB, D], F32)
        zT = sb("zT", [P, NP], F32)
        znode = zT[:, :].rearrange("p (b d) -> p b d", d=D)
        stats = sb("stats", [P, NB, 6], F32)
        mv = sb("mv", [P, NB, 2], F32)
        rstd = sb("rstd", [P, NB], F32)
        root = sb("root", [P, 2, NB], F32)
        nmr = sb("nmr", [P, NB], F32)
        small = sb("small", [P, 16], F32)
        smalli = sb("smalli", [P, 2], I32)
        rows = sb("rows", [P, 12, D], F32)
        colp = sb("colp", [P, 16], F32)

        scr_w = nc.dram_tensor("scr_windows", [1, JR], I32, kind="Internal").ap()
        scr_i = nc.dram_tensor("scr_index", [P, 2, JR], I32, kind="Internal").ap()
        scr_c = nc.dram_tensor("scr_code", [P, JR], F32, kind="Internal").ap()
        table1 = nc.dram_tensor("table1", [NP, 2 * D], F16, kind="Internal").ap()
        table2 = nc.dram_tensor("table2", [NP * REL, 2 * D], F16, kind="Internal").ap()

        m0 = pool.do(lambda e: e.memset(ident[:, :], 0.0))
        m1 = pool.do(lambda e: e.affine_select(out=ident[:, :], in_=ident[:, :], compare_op=ALU.not_equal,
                                               fill=1.0, base=0, pattern=[[-1, P]], channel_multiplier=1), m0)
        t_ident = pool.do(lambda e: e.tensor_copy(ident16[:, :], ident[:, :]), m1)
        pool.do(lambda e: e.memset(ones_row[:, :], 1.0))
        t_const = pool.do(lambda e: e.memset(ones16[:, :], 1.0))

        ch_x, ch_p = channel("ch_x"), channel("ch_param")
        m2 = dve.do(lambda e: e.memset(xres[:, FULL, :], 0.0))

        ROW = {}
        for k, name in enumerate(["L0_gnn_b1", "L0_gnn_g1", "L0_gnn_beta1", "L0_gnn_b2", "L0_gnn_g2",
                                  "L0_gnn_beta2", "L0_gnn_b3", "L0_gnn_g3", "L0_gnn_beta3", "L1_gnn_b",
                                  "L3_gnn_b2"]):
            ROW[name] = rows[:, k, :]
            act.dma(rows[:, k, :], io[name].rearrange("(a d) -> a d", a=1).broadcast_to([P, D]), ch_p)
        COL = {}
        for k, name in enumerate(["L2_gnn_b1", "L2_gnn_g1", "L2_gnn_beta1", "L2_gnn_b2", "L2_gnn_g2",
                                  "L2_gnn_beta2"]):
            COL[name] = colp[:, k:k + 1]
            act.dma(colp[:, k:k + 1], io[name].rearrange("(d a) -> d a", a=1), ch_p)
        for h in range(HB):
            act.dma(colp[:, 8 + h:9 + h], io["L3_gnn_b1"][h * P:h * P + P].rearrange("(d a) -> d a", a=1), ch_p)
        t_param = act.dma(colp[:, 10:11], io["L2_gnn_eps"].rearrange("(a d) -> a d", a=1).broadcast_to([P, 1]), ch_p)

        adj_ctx = ExitStack()
        adj = sb("adj", [P, NB, NP], F16, adj_ctx)
        own = ExitStack()
        flat = adj[:, :, :].rearrange("p b n -> p (b n)").bitcast(F32)
        carved = [0]

        def carve(shape, dt=F32):
            n = 1
            for k in shape[1:]:
                n *= k
            v = flat[0:shape[0], carved[0]:carved[0] + n]
            carved[0] += n
            shape = list(shape)
            if dt == F16:
                shape[-1] *= 2
            if dt != F32:
                v = v.bitcast(dt)
            if len(shape) == 3:
                v = v.rearrange("p (a b) -> p a b", b=shape[2])
            if len(shape) == 4:
                v = v.rearrange("p (a b c) -> p a b c", b=shape[2], c=shape[3])
            assert carved[0] <= NB * NP // 2
            return v
        nlo = zT[:, 0:JA]
        code = zT[:, JA:2 * JA]
        wcol = zT[0:1, 2 * JA:2 * JA + JA // GA].bitcast(I32)
        tab_i = carve([P, 3, TB, P], I32)
        prev_i = carve([P, TB], I32)
        steps = carve([P, JA])
        steps16 = carve([P, JA // 2], F16)
        ends = carve([P, 4, TB])
        span = carve([P, 4, TB])
        tcol = carve([P, TB])
        tmp_i = carve([P, TB], I32)
        v_i = carve([P, 2, TB, P], I32)
        S_LO, S_HI, TYPE, D_LO, D_HI, TILE = 0, 1, 2, (3, 5), (4, 6), 7
        piece = carve([P, 8, TB, P // 2], F16)
        NPICK = 5
        pick = carve([P, 2 * NPICK, CH // 2], F16)
        exp_f = carve([P, 6, CH])
        out_i = carve([P, 2, CH], I32)
        out_c = carve([P, CH])
        wrow_i = carve([1, CH], I32)
        free_end = NB * NP // 2
        plan_end = carved[0]

        q0 = dve.do(lambda e: e.memset(tab_i[:, :, TFULL, :], 0))
        q1 = dve.do(lambda e: e.memset(tab_i[:, 1, TFULL, :], NP + 4095), q0)
        q2 = dve.do(lambda e: e.memset(prev_i[:, :], 0))
        ch_t = [channel(f"ch_tab{i}") for i in range(3)]
        t_tab = []
        for i, name in enumerate(["src", "dst", "edge_type_8"]):
            e1 = io[name]
            n0 = TFULL * P * P
            sp.dma(tab_i[:, i, 0:TFULL, :], e1[0:n0].rearrange("(b q e) -> q b e", q=P, e=P), ch_t[i])
            sp.dma(tab_i[0:TROWS, i, TFULL, :], e1[n0:n0 + TROWS * P].rearrange("(q e) -> q e", e=P), ch_t[i], q1)
            t_tab.append(sp.dma(tab_i[TROWS:TROWS + 1, i, TFULL, 0:TREST],
                                e1[n0 + TROWS * P:E].rearrange("(q e) -> q e", q=1), ch_t[i]))
        sp.dma(xres[:, 0:FULL, :], io["x"][0:FULL * P, :].rearrange("(b p) d -> p b d", p=P), ch_x)
        t_x = sp.dma(xres[0:TAILN, FULL, :], io["x"][FULL * P:N, :], ch_x, m2)
        ch_v = channel("ch_prev")
        dst2 = io["dst"][0:(E // P) * P].rearrange("(t e) -> t e", e=P)[:, P - 1:P]
        act.dma(prev_i[1:P, 0:1], dst2[0:P - 1, :], ch_v, q2, allow_slow_non_contiguous=True)
        for b in range(1, TB):
            n = min(P, T - b * P)
            t_prev = act.dma(prev_i[0:n, b:b + 1], dst2[b * P - 1:b * P - 1 + n, :], ch_v,
                             allow_slow_non_contiguous=True)

        i0 = pool.do(lambda e: e.iota(steps[:, :], pattern=[[1, JA]], base=0, channel_multiplier=0,
                                      allow_small_or_imprecise_dtypes=True))
        i1 = pool.do(lambda e: e.iota(tcol[:, :], pattern=[[P, TB]], base=0, channel_multiplier=1,
                                      allow_small_or_imprecise_dtypes=True))
        t_zero_rest = pool.do(lambda e: e.memset(flat[:, plan_end:free_end], 0.0))
        i2 = dve.do(lambda e: e.tensor_copy(steps16[:, :], steps[:, :]), i0)
        c0 = dve.last()
        dve.wait(i1, t_prev, *t_tab)
        tile3 = tcol[:, :].unsqueeze(2).broadcast_to([P, TB, P])
        dve.do(lambda e: e.tensor_copy(piece[:, TYPE, :, :], tab_i[:, 2, :, :]))
        dve.do(lambda e: e.tensor_copy(piece[:, TILE, :, :], tile3))

        def low_high(v, lo, hi):
            a = dve.do(lambda e: e.tensor_scalar(v_i[:, 1, :, :], v, P - 1, None, ALU.bitwise_and), dve.last())
            dve.do(lambda e: e.tensor_copy(piece[:, lo, :, :], v_i[:, 1, :, :]), a)
            return dve.do(lambda e: e.tensor_tensor(piece[:, hi, :, :], v, v_i[:, 1, :, :], ALU.subtract), a)

        low_high(tab_i[:, 0, :, :], S_LO, S_HI)
        for k, lg in ((0, WA_LOG2), (1, WR_LOG2)):
            a = dve.do(lambda e, lg=lg: e.tensor_scalar(tmp_i[:, :], tab_i[:, 1, :, P - 1], lg, None,
                                                        ALU.logical_shift_right), c0, dve.last())
            a = dve.do(lambda e, k=k: e.tensor_tensor(ends[:, 2 * k, :], tmp_i[:, :], tcol[:, :], ALU.add), a, i1)
            a = dve.do(lambda e, lg=lg: e.tensor_scalar(tmp_i[:, :], prev_i[:, :], lg, None,
                                                        ALU.logical_shift_right), a)
            a = dve.do(lambda e, k=k: e.scalar_tensor_tensor(out=ends[:, 2 * k + 1, :], in0=tmp_i[:, :], scalar=-1.0,
                                                             in1=tcol[:, :], op0=ALU.add, op1=ALU.add), a)
            a = dve.do(lambda e, k=k, W=(WA, WR)[k]: e.scalar_tensor_tensor(
                out=v_i[:, 0, :, :], in0=tile3, scalar=float(W), in1=tab_i[:, 1, :, :], op0=ALU.mult, op1=ALU.add), a)
            low_high(v_i[:, 0, :, :], D_LO[k], D_HI[k])
        a = dve.do(lambda e: e.memset(ends[0:1, 1:4:2, 0:1], -1.0), dve.last())
        b_ = dve.do(lambda e: e.tensor_tensor(span[:, 0:4:2, :], ends[:, 0:4:2, :], ends[:, 1:4:2, :], ALU.add), a)
        b_ = dve.do(lambda e: e.tensor_scalar(span[:, 0:4:2, :], span[:, 0:4:2, :], -0.5, -0.5, ALU.mult, ALU.add), b_)
        a = dve.do(lambda e: e.tensor_tensor(span[:, 1:4:2, :], ends[:, 0:4:2, :], ends[:, 1:4:2, :], ALU.subtract), a)
        t_ends = dve.do(lambda e: e.tensor_scalar(span[:, 1:4:2, :], span[:, 1:4:2, :], 0.5, None, ALU.mult), a, b_)

        ch_s = channel("ch_plan")
        pick_free = [None] * NPICK
        state = {"store": None, ("psum", 0): None, ("psum", 1): None}

        def expand(k, a0, n, side, w):
            W = (WA, WR)[k]
            banks = bank[4 * side:4 * side + 4]
            st = steps[:, a0:a0 + n]
            PLACE, GE, IN, WIN, X, Y = (exp_f[:, i, 0:n] for i in range(6))
            dve.wait(w, dve.last())
            p_ = dve.do(lambda e, PLACE=PLACE, st=st, W=W, n=n: e.scalar_tensor_tensor(
                out=PLACE, in0=st, scalar=-float(W), in1=banks[2][:, 0:n], op0=ALU.mult, op1=ALU.add))
            w_ = dve.do(lambda e, WIN=WIN, st=st, n=n: e.scalar_tensor_tensor(
                out=WIN, in0=banks[3][:, 0:n], scalar=-1.0, in1=st, op0=ALU.mult, op1=ALU.add))
            g_ = dve.do(lambda e, GE=GE, PLACE=PLACE: e.tensor_scalar(GE, PLACE, 0.0, None, ALU.is_ge), p_)
            in_ = dve.do(lambda e, IN=IN, PLACE=PLACE, GE=GE, W=W: e.scalar_tensor_tensor(
                out=IN, in0=PLACE, scalar=float(W), in1=GE, op0=ALU.is_lt, op1=ALU.mult), g_)
            if k == 0:
                dve.do(lambda e, n=n, a0=a0: e.tensor_scalar(nlo[:, a0:a0 + n], banks[0][:, 0:n], -1.0, None, ALU.mult))
                x_ = dve.do(lambda e, n=n, X=X, PLACE=PLACE: e.scalar_tensor_tensor(
                    out=X, in0=banks[1][:, 0:n], scalar=float(WA * GA) / P, in1=PLACE, op0=ALU.mult, op1=ALU.add), in_)
                state["psum", side] = x_
                two = WIN.rearrange("p (a b) -> p a b", b=GA)
                y_ = dve.do(lambda e, Y=Y, two=two, n=n: e.tensor_tensor(
                    Y.rearrange("p (a b) -> p a b", b=GA), two, two[:, :, 0:1].broadcast_to([P, n // GA, GA]),
                    ALU.subtract), w_)
                x_ = dve.do(lambda e, X=X, Y=Y: e.scalar_tensor_tensor(out=X, in0=Y, scalar=float(WA), in1=X,
                                                                       op0=ALU.mult, op1=ALU.add), y_, x_)
                x_ = dve.do(lambda e, X=X, Y=Y, IN=IN: e.scalar_tensor_tensor(
                    out=Y, in0=X, scalar=1.0, in1=IN, op0=ALU.add, op1=ALU.mult), x_)
                dve.do(lambda e, Y=Y, a0=a0, n=n: e.tensor_scalar(code[:, a0:a0 + n], Y, -1.0, None, ALU.add), x_)
                dve.do(lambda e, WIN=WIN, a0=a0, n=n: e.tensor_scalar(
                    wcol[:, a0 // GA:(a0 + n) // GA], WIN[0:1, 0:n:GA], float(WA), None, ALU.mult))
            else:
                dve.do(lambda e, n=n: e.tensor_copy(out_i[:, 0, 0:n], banks[0][:, 0:n]), state["store"])
                y_ = dve.do(lambda e, n=n, Y=Y: e.tensor_copy(Y, banks[1][:, 0:n]))
                x_ = dve.do(lambda e, n=n, X=X, PLACE=PLACE: e.scalar_tensor_tensor(
                    out=X, in0=PLACE, scalar=float(REL), in1=banks[1][:, 0:n], op0=ALU.mult, op1=ALU.add), in_)
                state["psum", side] = dve.do(lambda e, n=n, Y=Y: e.scalar_tensor_tensor(
                    out=out_i[:, 1, 0:n], in0=banks[0][:, 0:n], scalar=float(REL), in1=Y, op0=ALU.mult,
                    op1=ALU.add), y_)
                x_ = dve.do(lambda e, X=X, GE=GE, IN=IN: e.scalar_tensor_tensor(
                    out=GE, in0=X, scalar=1.0, in1=IN, op0=ALU.add, op1=ALU.mult), x_)
                dve.do(lambda e, GE=GE, n=n: e.tensor_scalar(out_c[:, 0:n], GE, -1.0, None, ALU.add), x_)
                g = dve.do(lambda e, WIN=WIN, n=n: e.tensor_copy(wrow_i[:, 0:n], WIN[0:1, :]))
                sp.dma(scr_i[:, :, a0:a0 + n], out_i[:, :, 0:n], ch_s, g)
                sp.dma(scr_c[:, a0:a0 + n], out_c[:, 0:n], ch_s)
                state["store"] = sp.dma(scr_w[:, a0:a0 + n], wrow_i[:, 0:n], ch_s)

        npick, side, pending = 0, 1, None
        for k, J in ((1, JR), (0, JA)):
            for a0 in range(0, J, CH):
                n = min(CH, J - a0)
                side = 1 - side
                if k == 0:
                    sums_of = {0: [S_LO], 1: [S_HI], 2: [D_LO[0], D_HI[0]], 3: [TILE]}
                else:
                    sums_of = {0: [S_LO, S_HI], 1: [TYPE], 2: [D_LO[1], D_HI[1]], 3: [TILE]}
                for b in range(TB):
                    rws = P if b < TFULL else TLAST
                    s = npick % NPICK
                    u = act.do(lambda e, s=s, k=k, b=b, a0=a0, n=n: e.activation(
                        pick[:, 2 * s, 0:n], steps16[:, a0:a0 + n], ACT.Abs, bias=span[:, 2 * k, b:b + 1], scale=1.0),
                        t_ends, i2, pick_free[s])
                    v = dve.do(lambda e, s=s, k=k, b=b, n=n: e.tensor_scalar(
                        pick[:, 2 * s + 1, 0:n], pick[:, 2 * s, 0:n], span[:, 2 * k + 1, b:b + 1], None, ALU.is_lt), u)
                    pe.wait(v, state["psum", side])
                    for i, kinds in sums_of.items():
                        for q in kinds:
                            f = lambda e, i=i, q=q, s=s, n=n, b=b, r=rws, kinds=kinds, side=side: e.matmul(
                                bank[4 * side + i][:, 0:n], piece[0:r, q, b, :], pick[0:r, 2 * s + 1, 0:n],
                                start=(b == 0 and q == kinds[0]), stop=(b == TB - 1 and q == kinds[-1]))
                            if q == TILE:
                                w = pe.do(f)
                            else:
                                pe.quiet(f)
                    pick_free[s] = w
                    npick += 1
                    if b == NPICK - 1 and pending:
                        expand(*pending)
                pending = (k, a0, n, side, w)
        expand(*pending)
        store_free = state["store"]
        t_plan = dve.last()
        cut = plan_end // 2
        t_zero = [pool.do(lambda e: e.memset(flat[:, cut:plan_end], 0.0), t_plan, store_free),
                  dve.do(lambda e: e.memset(flat[:, 0:cut], 0.0), t_plan, store_free, pe.last()), t_zero_rest]

        LG = 2 * GA
        NLO, NHI, NST = 4, 8, 2
        AHEAD_LO = 2
        AHEAD_HI = 6
        NC = NB * WA * GA
        NG_LO = JA // LG
        assert JA % LG == 0
        iota = sb("iota", [P, NC], F16, own)
        minus_iota = sb("minus_iota", [P, P], F16, own)
        dist = sb("dist", [P, 2, LG * P], F16, own)
        lo_hot = sb("lo_hot", [P, NLO, LG, P], F16, own)
        hi_hot = sb("hi_hot", [P, NHI, NC], F16, own)
        stage = sb("stage", [P, NST, 2, NC], F16, own)
        t_iota = pool.do(lambda e: e.iota(iota[:, :], pattern=[[1, NC]], base=0, channel_multiplier=0,
                                          allow_small_or_imprecise_dtypes=True), t_plan, store_free)
        t_minus = pool.do(lambda e: e.iota(minus_iota[:, :], pattern=[[-1, P]], base=0, channel_multiplier=0,
                                           allow_small_or_imprecise_dtypes=True))
        regs = {}
        mm_tok, hi_tok, add_tok, stage_tok = [], [], [], []
        lo_tok, dist_tok, relu_tok = {}, {}, {}

        def by_act(g):
            return g * ACT_SHARE[0] % ACT_SHARE[1] < ACT_SHARE[0]

        act_groups = [g for g in range(NG_LO) if by_act(g)]
        turn_of = {g: i for i, g in enumerate(act_groups)}

        def distances(g, k):
            i = turn_of[g]
            j = g * LG + k
            dist_tok[g] = act.do(lambda e: e.activation(dist[:, i % 2, k * P:(k + 1) * P], iota[:, 0:P], ACT.Abs,
                                                        bias=nlo[:, j:j + 1], scale=1.0),
                                 t_iota, t_plan, relu_tok.get(act_groups[i - 2]) if i >= 2 else None)

        def low_hots(g):
            free = mm_tok[(g - NLO + 1) * LG - 1] if g >= NLO else None
            if by_act(g):
                lo_tok[g] = relu_tok[g] = act.do(lambda e: e.activation(
                    lo_hot[:, g % NLO, :, :].rearrange("p k i -> p (k i)"), dist[:, turn_of[g] % 2, :], ACT.Relu,
                    bias=1.0, scale=-1.0), dist_tok[g], free)
            else:
                for k in range(LG):
                    j = g * LG + k
                    lo_tok[g] = pool.do(lambda e, j=j, k=k: e.tensor_scalar(
                        lo_hot[:, g % NLO, k, :], minus_iota[:, :], nlo[:, j:j + 1], None, ALU.is_equal),
                        *((t_minus, t_plan, free) if k == 0 else ()))

        def high_hot(j):
            if j < JA:
                s = j % NHI
                hi_tok.append(dve.do(lambda e: e.tensor_scalar(hi_hot[:, s, :], iota[:, :], code[:, j:j + 1], None,
                                                               ALU.is_equal),
                                     t_iota, t_plan, mm_tok[j - NHI] if j >= NHI else None))

        def add(k):
            if k % REGS == 0:
                n = min(REGS, JA // GA - k)

                def load(e):
                    if not regs:
                        regs["dve"] = [e.alloc_register(f"window{i}") for i in range(REGS)]
                    e.load(regs["dve"][0:n], wcol[0:1, k:k + n])
                dve.quiet(load)

            def emit(e):
                c = e.snap(regs["dve"][k % REGS], min_val=0, max_val=NP - WA * GA)
                a = adj[:, :, bass.ds(c, WA * GA)]
                return e.tensor_tensor(a, a, stage[:, k // 2 % NST, k % 2, :].rearrange("p (h w) -> p h w", w=WA * GA),
                                       ALU.add)
            add_tok.append(dve.do(emit, stage_tok[k // 2], add_tok[k - 1] if k else None, *t_zero))

        for g in act_groups[:2]:
            for k in range(LG):
                distances(g, k)
        for g in range(AHEAD_LO):
            low_hots(g)
        for j in range(AHEAD_HI):
            high_hot(j)
        due = [(act_groups[2], k) for k in range(LG)]
        reach = 2
        for g in range(NG_LO + 1):
            if g < NG_LO:
                for m in range(LG):
                    j, q = g * LG + m, m % GA
                    ps = pair[g % 4][:, m // GA * CH:m // GA * CH + NC]
                    mm_tok.append(pe.do(lambda e, j=j, ps=ps, q=q: e.matmul(
                        ps, lo_hot[:, j // LG % NLO, j % LG, :], hi_hot[:, j % NHI, :], start=(q == 0),
                        stop=(q == GA - 1)), lo_tok[g], hi_tok[j], stage_tok[g - 4] if g >= 4 else None))
                    if m % GA == 0 and g:
                        high_hot(j + AHEAD_HI)
                        high_hot(j + 1 + AHEAD_HI)
                        add(2 * (g - 1) + m // GA)
                    elif m % GA == 0:
                        high_hot(j + AHEAD_HI)
                        high_hot(j + 1 + AHEAD_HI)
                if g + AHEAD_LO < NG_LO:
                    low_hots(g + AHEAD_LO)
                    if by_act(g + AHEAD_LO) and reach + 1 < len(act_groups):
                        reach += 1
                        due += [(act_groups[reach], k) for k in range(LG)]
                for item in due[:2]:
                    distances(*item)
                due = due[2:]
                stage_tok.append(act.do(lambda e, g=g: e.activation(
                    stage[:, g % NST, :, :], pair[g % 4][:, :].rearrange("p (h c) -> p h c", h=2)[:, :, 0:NC], ACT.Copy),
                    mm_tok[-1], add_tok[2 * (g - NST) + 1] if g >= NST else None))
            else:
                add(2 * (g - 1))
                add(2 * (g - 1) + 1)
        own.close()
        for b in range(NB):
            t_self = dve.do(lambda e, b=b: e.tensor_tensor(adj[:, b, b * P:b * P + P], adj[:, b, b * P:b * P + P],
                                                           ident16[:, :], ALU.add), add_tok[-1], t_ident)
        adj_ready = t_self

        dense = ExitStack()
        split = sb("split", [P, NB, 2, D], F16, dense)
        hT = split[:, :, :, :].rearrange("p b s d -> p (b s d)").bitcast(F32)
        weights = sb("weights", [P, 7, D], F32, dense)
        deg = sb("deg", [P, NB], F32, dense)
        dinv = sb("dinv", [P, NB], F32, dense)
        ch_w = channel("ch_weights")
        WT = {}
        for k, name in enumerate(["L0_gnn_W1", "L0_gnn_W2", "L0_gnn_W3", "L1_gnn_W", "L2_gnn_W1", "L2_gnn_W2"]):
            WT[name] = weights[:, k, :]
            t_w = sp.dma(weights[:, k, :], io[name], ch_w, t_self)

        def turn(ready, solo=0):
            k = 0
            freed = [None] * 6
            row_done = []
            for i in range(NB + 1):
                row = []
                pieces = [] if i == NB else [(i, 1)] + [(j0, min(8, NB - j0)) for j0 in range(i + 1, NB, 8)]
                for j0, n in pieces:
                    pa, pb = 2 * k % 6, (2 * k + 1) % 6
                    k += 1
                    va, vb = bank[pa].bitcast(F16), bank[pb].bitcast(F16)
                    pe.wait(ready, t_ident, freed[pa], freed[pb])
                    for m in range(n):
                        f = lambda e, m=m, j=j0 + m, i=i, va=va: e.transpose(
                            va[:, m * P:m * P + P], adj[:, i, j * P:j * P + P], ident16[:, :])
                        if j0 == i:
                            w2 = pe.do(f)
                        else:
                            pe.quiet(f)
                    if j0 != i:
                        for m in range(n):
                            f = lambda e, m=m, j=j0 + m, i=i, vb=vb: e.transpose(
                                vb[:, m * P:m * P + P], adj[:, j, i * P:i * P + P], ident16[:, :])
                            if m == n - 1:
                                w2 = pe.do(f)
                            else:
                                pe.quiet(f)
                    if k > solo and (j0 == i or k % 3 == 0):
                        freed[pa] = dve.do(lambda e, i=i, j0=j0, n=n, va=va: e.tensor_copy(
                            adj[:, j0:j0 + n, i * P:i * P + P], va[:, 0:n * P].rearrange("p (n q) -> p n q", q=P)), w2)
                    else:
                        freed[pa] = act.do(lambda e, i=i, j0=j0, n=n, va=va: e.activation(
                            adj[:, j0:j0 + n, i * P:i * P + P], va[:, 0:n * P].rearrange("p (n q) -> p n q", q=P),
                            ACT.Copy), w2)
                    if j0 != i and (k <= solo or k % 3 == 0):
                        freed[pb] = act.do(lambda e, i=i, j0=j0, n=n, vb=vb: e.activation(
                            adj[:, i, j0 * P:(j0 + n) * P], vb[:, 0:n * P], ACT.Copy), w2)
                    elif j0 != i:
                        freed[pb] = dve.do(lambda e, i=i, j0=j0, n=n, vb=vb: e.tensor_copy(
                            adj[:, i, j0 * P:(j0 + n) * P], vb[:, 0:n * P]), w2)
                    row += [freed[pa], freed[pb]]
                row_done.append(row)
                if i:
                    b = i - 1
                    pe.wait(*row_done[b], t_const)
                    for h in range(NB):
                        f = lambda e, b=b, h=h: e.matmul(bank[7][:, b:b + 1], adj[:, h, b * P:b * P + P], ones16[:, :],
                                                         start=(h == 0), stop=(h == NB - 1))
                        if b == NB - 1 and h == NB - 1:
                            w = pe.do(f)
                        else:
                            pe.quiet(f)
            return w, [act.last(), dve.last()]

        def take_degrees(ready):
            return dve.do(lambda e: e.tensor_copy(deg[:, :], bank[7][:, 0:NB]), ready)

        def aggregate(ready, block_ready, unscale, eps_rhs=None):
            pe.wait(*ready)
            summed_ = {}
            for k in range(NB):
                pe.wait(*block_ready[k])
                for s in range(2):
                    for c, (c0, n) in enumerate(chunk):
                        last = k == NB - 1 and s == 1
                        f = lambda e, k=k, s=s, c=c, c0=c0, n=n, last=last: e.matmul(
                            bank[c][:, 0:n], split[:, k, s, :], adj[:, k, c0:c0 + n],
                            start=(k == 0 and s == 0), stop=last)
                        if last:
                            summed_[c] = pe.do(f)
                        else:
                            pe.quiet(f)
                    if eps_rhs is not None and k == NB - 1 and s == 0:
                        for b in range(NB):
                            pe.quiet(lambda e, b=b: e.matmul(
                                bank[b * P // CH][:, b * P % CH:b * P % CH + P], xres[:, b, :], eps_rhs,
                                start=False, stop=False, skip_group_check=True))
            func = ACT.Copy if isinstance(unscale, float) else ACT.Identity
            toks = []
            for c, (c0, n) in enumerate(chunk):
                if c % 2:
                    toks.append(dve.do(lambda e, c=c, c0=c0, n=n: e.tensor_scalar(
                        zT[:, c0:c0 + n], bank[c][:, 0:n], unscale, None, ALU.mult), summed_[c]))
                else:
                    toks.append(act.do(lambda e, c=c, c0=c0, n=n: e.activation(
                        zT[:, c0:c0 + n], bank[c][:, 0:n], func, scale=unscale), summed_[c]))
            return toks

        def project(z, ready, W, fold):
            pe.wait(*ready)
            for i, quad in enumerate(quads):
                pe.wait(z[i])
                for b in quad:
                    w = pe.do(lambda e, b=b, i=i: e.matmul(bank[i][:, b % 4 * P:b % 4 * P + P], zT[:, b * P:b * P + P], W,
                                                           start=True, stop=True))
                folded = {b: fold(b, bank[i][:, b % 4 * P:b % 4 * P + P], w) for b in quad}
                t = stats_of(znode, quad, folded)
            return t

        def rsqrt(to, var, eps, ready):
            n = to.shape[1]
            v, r = root[:, 0, 0:n], root[:, 1, 0:n]
            a = dve.do(lambda e: e.tensor_scalar(v, var, eps, None, ALU.add), ready)
            a = act.do(lambda e: e.activation(r, v, ACT.Sqrt), a)
            a = dve.do(lambda e: e.reciprocal(to, r), a)
            a = dve.do(lambda e: e.tensor_tensor(r, to, to, ALU.mult), a)
            a = dve.do(lambda e: e.tensor_tensor(r, r, v, ALU.mult), a)
            a = dve.do(lambda e: e.tensor_scalar(r, r, -0.5, 1.5, ALU.mult, ALU.add), a)
            return dve.do(lambda e: e.tensor_tensor(to, to, r, ALU.mult), a)

        quads = [range(b, min(b + 4, NB)) for b in range(0, NB, 4)]

        def stats_of(src, quad, ready):
            for b in quad:
                a = dve.do(lambda e, b=b: e.bn_stats(stats[:, b, :], src[:, b, :]), ready[b])
            for b in quad:
                c = dve.do(lambda e, b=b: e.bn_aggr(mv[:, b, :], stats[:, b, :]), a)
            return c

        def norm_params(ready):
            d = rsqrt(rstd[:, :], mv[:, :, 1], EPS, ready)
            return dve.do(lambda e: e.scalar_tensor_tensor(out=nmr[:, :], in0=mv[:, :, 0], scalar=-1.0, in1=rstd[:, :],
                                                           op0=ALU.mult, op1=ALU.mult), d)

        def normalize(dst, src, quad, ready, both=True):
            last = {}
            for b in quad:
                if b % 2 and both:
                    last[1] = act.do(lambda e, b=b: e.activation(dst[:, b, :], src[:, b, :], ACT.Identity,
                                                                 bias=nmr[:, b:b + 1], scale=rstd[:, b:b + 1]), ready)
                else:
                    last[0] = dve.do(lambda e, b=b: e.tensor_scalar(dst[:, b, :], src[:, b, :], rstd[:, b:b + 1],
                                                                    nmr[:, b:b + 1], ALU.mult, ALU.add), ready)
            return list(last.values())

        def norm_all(dst, src, ready, both=True):
            for quad in quads:
                t = stats_of(src, quad, ready)
            t = norm_params(t)
            done_ = {}
            for quad in quads:
                n = normalize(dst, src, quad, t, both)
                for b in quad:
                    done_[b] = n
            return done_

        def bcast(row, n=NB):
            return row.unsqueeze(1).broadcast_to([P, n, D])

        def percol(col):
            return col.unsqueeze(2).broadcast_to([P, col.shape[1], D])

        def split_parts(src, quad, scale, ready):
            q0, q1 = quad[0], quad[-1] + 1
            hi = act.do(lambda e: e.activation(split[:, q0:q1, 0, :], src[:, q0:q1, :],
                                               ACT.Copy if isinstance(scale, float) else ACT.Identity, scale=scale), *ready)
            lo = dve.do(lambda e: e.scalar_tensor_tensor(out=split[:, q0:q1, 1, :], in0=src[:, q0:q1, :], scalar=scale,
                                                         in1=split[:, q0:q1, 0, :], op0=ALU.mult, op1=ALU.subtract), hi)
            return [hi, lo]

        t_deg, turned = turn(adj_ready)
        t_deg = take_degrees(t_deg)
        t_dinv = rsqrt(dinv[:, :], deg[:, :], 0.0, t_deg)

        def power_scale(k, top, ready):
            d = dve.do(lambda e: e.tensor_scalar(small[:, k:k + 1], top, 2.0 ** -100, 2.0 ** 110, ALU.max, ALU.min), ready)
            d = dve.do(lambda e: e.tensor_scalar(smalli[:, 0:1], small[:, k:k + 1].bitcast(I32), 0x7F800000, None,
                                                 ALU.bitwise_and), d)
            d = dve.do(lambda e: e.tensor_scalar(small[:, k + 1:k + 2], smalli[:, 0:1].bitcast(F32), 2.0 ** -14, None,
                                                 ALU.mult), d)
            return dve.do(lambda e: e.reciprocal(small[:, k:k + 1], small[:, k + 1:k + 2]), d)

        b_ = dve.do(lambda e: e.tensor_reduce(small[:, 6:7], xres[:, :, :].rearrange("p b d -> p (b d)"), AX.X, ALU.max,
                                              apply_absolute_value=True), t_x)
        b_ = pool.do(lambda e: e.partition_all_reduce(small[:, 7:8], small[:, 6:7], P, bass.bass_isa.ReduceOp.max), b_)
        scaled_ready = {1: power_scale(0, small[:, 7:8], b_)}
        for layer in (1, 2):
            for q, name in enumerate((f"L0_gnn_g{layer}", f"L0_gnn_beta{layer}")):
                b_ = dve.do(lambda e, q=q, name=name: e.tensor_reduce(small[:, 8 + q:9 + q], ROW[name], AX.X, ALU.max,
                                                                      apply_absolute_value=True), dve.last(), t_param)
            b_ = dve.do(lambda e: e.scalar_tensor_tensor(out=small[:, 10:11], in0=small[:, 8:9], scalar=float(D) ** 0.5,
                                                         in1=small[:, 9:10], op0=ALU.mult, op1=ALU.add), b_)
            scaled_ready[layer + 1] = power_scale(2 * layer, small[:, 10:11], b_)

        block_ready = {}
        for quad in quads:
            q0, q1 = quad[0], quad[-1] + 1
            a = dve.do(lambda e, q0=q0, q1=q1: e.tensor_tensor(znode[:, q0:q1, :], xres[:, q0:q1, :],
                                                               percol(dinv[:, q0:q1]), ALU.mult), t_dinv)
            t = split_parts(znode, quad, small[:, 0:1], [a, *scaled_ready.values()])
            block_ready.update({b: t for b in quad})
        for layer in (1, 2, 3):
            W, bias = WT[f"L0_gnn_W{layer}"], ROW[f"L0_gnn_b{layer}"]
            gain, beta = ROW[f"L0_gnn_g{layer}"], ROW[f"L0_gnn_beta{layer}"]
            z = aggregate(turned, block_ready, small[:, 2 * layer - 1:2 * layer])

            def fold(b, ps, w, bias=bias):
                return dve.do(lambda e: e.scalar_tensor_tensor(out=znode[:, b, :], in0=ps, scalar=dinv[:, b:b + 1],
                                                               in1=bias, op0=ALU.mult, op1=ALU.add), w)
            t = project(z, [t_w], W, fold)
            p = norm_params(t)
            block_ready = {}
            for quad in quads:
                q0, q1 = quad[0], quad[-1] + 1
                zq, n = znode[:, q0:q1, :], q1 - q0
                a = normalize(znode, znode, quad, p, layer < 3)
                a = dve.do(lambda e, g=gain, zq=zq, n=n: e.tensor_tensor(zq, zq, bcast(g, n), ALU.mult), *a)
                a = dve.do(lambda e, g=beta, zq=zq, n=n: e.tensor_tensor(zq, zq, bcast(g, n), ALU.add), a)
                if layer < 3:
                    a = dve.do(lambda e, zq=zq, q0=q0, q1=q1: e.scalar_tensor_tensor(
                        out=zq, in0=zq, scalar=0.0, in1=percol(dinv[:, q0:q1]), op0=ALU.max, op1=ALU.mult), a)
                    s_ = split_parts(znode, quad, small[:, 2 * layer:2 * layer + 1], [a])
                    block_ready.update({b: s_ for b in quad})
                else:
                    a = dve.do(lambda e, zq=zq, q0=q0, q1=q1: e.scalar_tensor_tensor(
                        out=zq, in0=zq, scalar=0.0, in1=xres[:, q0:q1, :], op0=ALU.max, op1=ALU.add), a)
                    t = stats_of(znode, quad, {b: a for b in quad})
        l0_projected = p

        def next_stream(t, scale=FX):
            p = norm_params(t)
            ready, xr_ = {}, {}
            for quad in quads:
                n = normalize(xres, znode, quad, p)
                xr_.update({b: n for b in quad})
                s_ = split_parts(xres, quad, scale, n)
                ready.update({b: s_ for b in quad})
            return xr_, ready
        t_cnt, back = turn(l0_projected, solo=18)
        x_blocks, block_ready = next_stream(t)
        t_cnt = take_degrees(t_cnt)
        z = aggregate(back, block_ready, 1.0 / FX)
        tr = pe.do(lambda e: e.transpose(bank[7][:, 0:P], WT["L1_gnn_W"], ident[:, :]), t_cnt)
        tr = dve.do(lambda e: e.tensor_copy(weights[:, 6, :], bank[7][:, 0:P]), tr)

        def fold1(b, ps, w):
            a = dve.do(lambda e: e.scalar_tensor_tensor(out=znode[:, b, :], in0=ROW["L1_gnn_b"], scalar=deg[:, b:b + 1],
                                                        in1=ps, op0=ALU.mult, op1=ALU.add), w, t_cnt)
            return dve.do(lambda e: e.tensor_tensor(znode[:, b, :], znode[:, b, :], xres[:, b, :], ALU.add), a, *x_blocks[b])
        t = project(z, [tr], weights[:, 6, :], fold1)
        t_eps_free = pe.last()

        eps_id = weights[:, 6, :]
        ei = dve.do(lambda e: e.tensor_scalar(eps_id, ident[:, :], colp[:, 10:11], FX, ALU.mult, ALU.mult), t_eps_free, t_param)
        x_blocks, block_ready = next_stream(t)
        z = aggregate([ei], block_ready, 1.0 / FX, eps_id)
        adj_free = pe.last()
        rel = ExitStack()
        carved[0] = 0
        NG = 6
        sums = carve([P, NW4, G, D + 1])
        gath = carve([P, NG, D + 1], F16)
        hot = carve([P, NG, G * P // 2], F16)
        iota_r = carve([P, G * P // 2], F16)
        index = carve([P, 2, JR], I32)
        code_r = carve([P, JR])
        win = carve([1, JR], I32)
        place = carve([P, REL, P])
        inv = carve([P, NW4 * G])
        RR = REL + 1
        w1 = carve([P, RR * H])
        w2 = carve([P, HB * RR * D])
        w1_r = w1.rearrange("p (r o) -> p r o", o=H)
        w2_r = w2.rearrange("p (h r d) -> p h r d", r=RR, d=D)
        ones_all = carve([P, P])
        parts = carve([P, 2, REL * 2, D // 2], F16)

        ch_l3, ch_l4 = channel("ch_l3"), channel("ch_l4")
        sp.wait(adj_free, store_free)
        sp.dma(index[:, :, :], scr_i, ch_l3)
        sp.dma(code_r[:, :], scr_c, ch_l3)
        t_lists = sp.dma(win[:, :], scr_w, ch_l3)
        sp.dma(w1_r[:, 0:REL, :], io["L3_gnn_W1"].rearrange("r k o -> k r o"), ch_l4)
        sp.dma(w1_r[:, REL, :], io["L3_gnn_root1"], ch_l4)
        for h in range(HB):
            sp.dma(w2_r[:, h, 0:REL, :], io["L3_gnn_W2"][:, h * P:h * P + P, :].rearrange("r k o -> k r o"), ch_l4)
        t_w3 = sp.dma(w2_r[:, :, REL, :], io["L3_gnn_root2"].rearrange("(h k) o -> k h o", k=P), ch_l4)

        pool.wait(adj_free)
        z0 = pool.do(lambda e: e.memset(gath[:, :, :], 1.0))
        z0 = pool.do(lambda e: e.iota(iota_r[:, :], pattern=[[1, G * P]], base=0, channel_multiplier=0,
                                      allow_small_or_imprecise_dtypes=True))
        z1 = pool.do(lambda e: e.memset(place[:, :, :], 1.0))
        z1 = pool.do(lambda e: e.affine_select(out=place[:, :, :], in_=place[:, :, :], compare_op=ALU.is_ge, fill=0.0,
                                               base=0, pattern=[[REL * GN, P // GN], [-REL, P]], channel_multiplier=1), z1)
        t_place = pool.do(lambda e: e.affine_select(out=place[:, :, :], in_=place[:, :, :], compare_op=ALU.is_ge, fill=0.0,
                                                    base=REL - 1, pattern=[[-REL * GN, P // GN], [REL, P]],
                                                    channel_multiplier=-1), z1)
        t_ones = pool.do(lambda e: e.memset(ones_all[:, :], 1.0))
        sums_zero = [pool.do(lambda e: e.memset(sums[:, :, :, :], 0.0))]

        cur, nxt = zT[:, :], hT
        ready = z
        bstat = stats[:, 0:NCH, :]
        for layer in (1, 2):
            W = WT[f"L2_gnn_W{layer}"]
            b_, g_, be_ = (COL[f"L2_gnn_{n}{layer}"] for n in ("b", "g", "beta"))
            for c, (c0, n) in enumerate(chunk):
                pe.wait(ready[c] if layer == 1 else ready[c // 4])
                w = pe.do(lambda e, c=c, c0=c0, n=n, cur=cur, W=W: e.matmul(bank[c][:, 0:n], W, cur[:, c0:c0 + n],
                                                                           start=True, stop=True))
                a = act.do(lambda e, c=c, c0=c0, n=n, nxt=nxt, b_=b_: e.activation(nxt[:, c0:c0 + n], bank[c][:, 0:n],
                                                                                   ACT.Identity, bias=b_, scale=1.0), w, t_param)
                m = min(n, N - c0)
                a = dve.do(lambda e, c=c, c0=c0, m=m, nxt=nxt: e.bn_stats(bstat[:, c, :], nxt[:, c0:c0 + m]), a)
            a = dve.do(lambda e: e.bn_aggr(mv[:, 0, :], bstat), a)
            a = rsqrt(small[:, 5:6], mv[:, 0, 1:2], EPS, a)
            a = dve.do(lambda e, g_=g_: e.tensor_tensor(small[:, 6:7], small[:, 5:6], g_, ALU.mult), a)
            a = dve.do(lambda e: e.tensor_tensor(small[:, 7:8], mv[:, 0, 0:1], small[:, 6:7], ALU.mult), a)
            a = dve.do(lambda e, be_=be_: e.tensor_tensor(small[:, 8:9], be_, small[:, 7:8], ALU.subtract), a)
            half = 4 * CH
            r1 = act.do(lambda e, nxt=nxt: e.activation(nxt[:, 0:half], nxt[:, 0:half], ACT.Relu, bias=small[:, 8:9],
                                                        scale=small[:, 6:7]), a)
            r2 = act.do(lambda e, nxt=nxt: e.activation(nxt[:, half:NP], nxt[:, half:NP], ACT.Relu, bias=small[:, 8:9],
                                                        scale=small[:, 6:7]), a)
            cur, nxt = nxt, cur
            ready = [r1, r2]
        toks = []
        for b in range(NB):
            c, o = b // 4 % 7, b % 4 * P
            w = pe.do(lambda e, b=b, c=c, o=o, cur=cur: e.transpose(bank[c][:, o:o + P], cur[:, b * P:b * P + P], ident[:, :]),
                      *ready)
            if b % 4 == 3 or b == NB - 1:
                b0 = b // 4 * 4
                n = b + 1 - b0
                toks = dve.do(lambda e, b0=b0, n=n: e.tensor_tensor(
                    xres[:, b0:b0 + n, :], xres[:, b0:b0 + n, :],
                    bank[b0 // 4 % 7][:, 0:n * P].rearrange("p (b d) -> p b d", d=P), ALU.add), w)
        for quad in quads:
            t = stats_of(xres, quad, {b: toks for b in quad})
        t = norm_params(t)
        ch_t1 = channel("ch_table1")
        x_ready = []
        for quad in quads:
            n = normalize(xres, xres, quad, t)
            x_ready += n
            q0, q1 = quad[0], quad[-1] + 1
            t_table1 = sp.dma(table1[q0 * P:q1 * P, :].rearrange("(b p) f -> p b f", p=P),
                              split[:, q0:q1, :, :].rearrange("p b q d -> p b (q d)"), ch_t1,
                              *split_parts(xres, quad, FX, [*n, *ready]))
        dense.close()
        w1p = sb("w1p", [P, 2, RR, H], F16, rel)
        w2p = w1.bitcast(F16).rearrange("p (q h r d) -> p q h r d", q=2, h=HB, r=RR)
        rowT = w2.bitcast(F16).rearrange("p (s q r n) -> p s q r n", s=2, q=2, r=RR)
        hTp = sb("hTp", [P, 2, 2, HB, P], F16, rel)
        h32 = sb("h32", [P, HB, P], F32, rel)
        bound = sb("bound", [P, 16], F32, rel)
        boundi = sb("boundi", [P, 4], I32, rel)
        scales = sb("scales", [P, 2, 4], F32, rel)
        unscale = sb("unscale", [P, 8], F32, rel)

        def two_parts(hi, lo, src, scale, ready):
            a = act.do(lambda e: e.activation(hi, src, ACT.Identity, scale=scale), *ready)
            return dve.do(lambda e: e.scalar_tensor_tensor(out=lo, in0=src, scalar=scale, in1=hi, op0=ALU.mult,
                                                           op1=ALU.subtract), a)

        ch_g = [channel(f"ch_gather{i}") for i in range(NG)]
        def relation_sums(table, which, factor, ready, between=()):
            between = list(between)
            NPAIR = 3
            gt, ht, mt, at = [], [], [], []
            pool.wait(*ready, t_lists, z0)
            dve.wait(*sums_zero, t_lists, z0)

            def gather(j):
                s = j % NG
                ch = ch_g[s]
                ch[1] += 16
                pool.wait(mt[j - NG] if j >= NG else None)
                pool.program.append(lambda e, s=s, j=j: e.indirect_dma_start(
                    gath[:, s, 0:2 * D], None, table,
                    bass.IndirectOffsetOnAxis(ap=index[:, which, j:j + 1].bitcast(U32), axis=0)).then_inc(ch_g[s][0], 16))
                gt.append((ch[0], ch[1]))

            def one_hot(j):
                s = j % NG
                ht.append(dve.do(lambda e, s=s, j=j: e.tensor_scalar(hot[:, s, :], iota_r[:, :], code_r[:, j:j + 1], None,
                                                                     ALU.is_equal), mt[j - NG] if j >= NG else None))

            for j in range(AHEAD):
                one_hot(j)
            for j in range(JR):
                s = j % NG
                gather(j)
                pe.wait(gt[j], ht[j], at[j - NPAIR] if j >= NPAIR else None)
                ps = pair[j % NPAIR]
                for g in range(G):
                    for q, (a, b) in enumerate([(D, 2 * D + 1), (0, D)]):
                        f = lambda e, g=g, q=q, a=a, b=b, s=s, ps=ps: e.matmul(
                            ps[:, g * CH // 2:g * CH // 2 + b - a], hot[:, s, g * P:g * P + P], gath[:, s, a:b],
                            start=(q == 0), stop=(q == 1), skip_group_check=True)
                        if g == G - 1 and q == 1:
                            m = pe.do(f)
                        else:
                            pe.quiet(f)
                mt.append(m)
                if j % REGS == 0:
                    n = min(REGS, JR - j)

                    def load(e, j=j, n=n):
                        e.load(regs["dve"][0:n], win[0:1, j:j + n])
                    dve.quiet(load)

                def add(e, j=j, ps=ps):
                    c = e.snap(regs["dve"][j % REGS], min_val=0, max_val=NW4 - 1)
                    a = sums[:, bass.ds(c, 1), :, :].rearrange("p o g d -> p (o g) d")
                    return e.tensor_tensor(a, a, ps[:, :].rearrange("p (g d) -> p g d", g=G)[:, :, 0:D + 1], ALU.add)
                at.append(dve.do(add, mt[j], at[j - 1] if j else None))
                if j + AHEAD < JR:
                    one_hot(j + AHEAD)
                if between and j >= REGS:
                    between.pop(0)()
            cnt = sums[:, :, :, D].rearrange("p w g -> p (w g)")
            a = dve.do(lambda e: e.tensor_scalar(inv[:, :], cnt, 1.0, None, ALU.max), at[-1])
            a = dve.do(lambda e: e.reciprocal(inv[:, :], inv[:, :]), a)
            return dve.do(lambda e: e.tensor_scalar(inv[:, :], inv[:, :], factor, None, ALU.mult), a)

        GB = WPB * G
        sums_g = sums[:, :, :, :].rearrange("p w g d -> p (w g) d")

        sq1, sqr = zT[:, 0:RR * H], zT[:, RR * H:RR * H + HB * D]
        sq2 = w1p.rearrange("p q r o -> p (q r o)").bitcast(F32)[:, 0:HB * REL * D]
        sqb = h32[:, 0, 0:HB]
        act.wait(t_w3, t_param, t_table1, *x_ready)
        act.do(lambda e: e.activation(sq1[:, :], w1[:, :], ACT.Square))
        act.do(lambda e: e.activation(sqb, colp[:, 8:8 + HB], ACT.Square))
        act.do(lambda e: e.activation(sqr.rearrange("p (h d) -> p h d", d=D), w2_r[:, :, REL, :], ACT.Square))
        t_sq = act.do(lambda e: e.activation(sq2.rearrange("p (h c) -> p h c", h=HB),
                                             w2_r[:, :, 0:REL, :].rearrange("p h r d -> p h (r d)"), ACT.Square))
        between, tok = [], {}

        def later(lane, emit, name, *needs):
            between.append(lambda: tok.update({name: lane.do(emit, *[tok[n] for n in needs if n])}))
        tok["sq"], tok["ones"] = t_sq, t_ones

        def square_sum(name, to, pieces, free=None):
            for i, v in enumerate(pieces):
                later(pe, lambda e, i=i, v=v: e.matmul(to[:, 0:v.shape[1]], ones_all[:, :], v, start=(i == 0),
                                                       stop=(i == len(pieces) - 1), skip_group_check=True),
                      name, "sq", "ones", free)

        def reduced(name, col, src, op, need):
            later(dve, lambda e: e.tensor_reduce(bound[:, col:col + 1], src, AX.X, op), name, need)

        W2C = REL * D
        assert W2C == 2 * CH
        square_sum("w1", bank[6], [sq1[:, c:c + H] for c in range(0, RR * H, H)])
        reduced("W1", 8, bank[6][:, 0:H], ALU.add, "w1")
        square_sum("b1", bank[7], [sqb])
        reduced("B1", 1, bank[7][:, 0:HB], ALU.add, "b1")
        later(dve, lambda e: e.scalar_tensor_tensor(out=bound[:, 2:3], in0=bound[:, 8:9], scalar=float(RR * D),
                                                    in1=bound[:, 1:2], op0=ALU.mult, op1=ALU.add), "H", "W1", "B1")
        for q, free in ((0, "B1"), (1, "W1")):
            square_sum(f"w2{q}", bank[7 - q], [sq2[:, h * W2C + q * CH:h * W2C + (q + 1) * CH] for h in range(HB)], free)
            reduced(f"max{q}", 3 + q, bank[7 - q][:, :], ALU.max, f"w2{q}")
            reduced(f"sum{q}", 5 + q, bank[7 - q][:, :], ALU.add, f"w2{q}")
        square_sum("r2", bank[7], [sqr], "sum0")
        reduced("R2", 7, bank[7][:, 0:HB * D], ALU.add, "r2")
        reduced("W2", 10, bound[:, 5:8], ALU.add, "R2")
        reduced("max", 0, bound[:, 3:5], ALU.max, "R2")
        later(dve, lambda e: e.tensor_scalar(bound[:, 9:10], bound[:, 2:3], 2.0, None, ALU.mult), "H2", "max")
        later(dve, lambda e: e.tensor_tensor(bound[:, 11:12], bound[:, 9:10], bound[:, 0:1], ALU.mult), "Y", "H2")
        later(act, lambda e: e.activation(bound[:, 12:16], bound[:, 8:12], ACT.Sqrt), "top", "Y")
        later(dve, lambda e: e.tensor_scalar(bound[:, 12:16], bound[:, 12:16], 2.0 ** -50, 2.0 ** 60, ALU.max, ALU.min),
              "top", "top")
        later(dve, lambda e: e.tensor_scalar(boundi[:, :], bound[:, 12:16].bitcast(I32), 0x7F800000, None,
                                             ALU.bitwise_and), "top", "top")
        later(dve, lambda e: e.tensor_scalar(scales[:, 1, :], boundi[:, :].bitcast(F32), 2.0 ** -14, None, ALU.mult),
              "top", "top")
        later(dve, lambda e: e.reciprocal(scales[:, 0, :], scales[:, 1, :]), "scale", "top")
        later(dve, lambda e: e.scalar_tensor_tensor(out=unscale[:, 0:1], in0=scales[:, 0, 1:2], scalar=1.0 / FX,
                                                    in1=scales[:, 1, 0:1], op0=ALU.mult, op1=ALU.mult), "u0", "scale")
        later(dve, lambda e: e.tensor_tensor(unscale[:, 1:2], scales[:, 1, 1:2], scales[:, 1, 2:3], ALU.mult), "u1", "scale")
        later(dve, lambda e: e.tensor_tensor(unscale[:, 2:3], unscale[:, 1:2], scales[:, 0, 3:4], ALU.mult), "u2", "u1")
        later(dve, lambda e: e.tensor_scalar(unscale[:, 4:4 + HB], colp[:, 8:8 + HB], scales[:, 0, 1:2], None, ALU.mult),
              "ub", "u2")
        later(act, lambda e: e.activation(w1p[:, 0, :, :].rearrange("p r o -> p (r o)"), w1[:, :], ACT.Identity,
                                          scale=scales[:, 0, 0:1]), "w1hi", "scale", "w21")
        for r in range(RR):
            later(dve, lambda e, r=r: e.scalar_tensor_tensor(
                out=w1p[:, 1, r, :], in0=w1_r[:, r, :], scalar=scales[:, 0, 0:1], in1=w1p[:, 0, r, :], op0=ALU.mult,
                op1=ALU.subtract), "w1lo", "w1hi")
        later(act, lambda e: e.activation(w2p[:, 0, :, :, :], w2_r[:, :, :, :], ACT.Identity, scale=scales[:, 0, 2:3]),
              "w2hi", "w1lo")
        for h in range(HB):
            for r in range(RR):
                later(dve, lambda e, h=h, r=r: e.scalar_tensor_tensor(
                    out=w2p[:, 1, h, r, :], in0=w2_r[:, h, r, :], scalar=scales[:, 0, 2:3], in1=w2p[:, 0, h, r, :],
                    op0=ALU.mult, op1=ALU.subtract), "w2lo", "w2hi")
        done = relation_sums(table1, 0, 1.0, [t_table1], between)
        t_weights = [tok["w1hi"], tok["w1lo"], tok["w2hi"], tok["w2lo"], tok["ub"]]
        PRODUCTS = ((1, 0), (0, 1), (0, 0))
        root_out = znode
        ch_t2 = [channel(f"ch_table2_{i}") for i in range(2)]
        rowT_free, hTp_free = [None, None], [None, None]
        bank_free = [None] * 8
        pe.wait(*t_weights)
        act.wait(*t_weights)
        dve.wait(*t_weights)
        part_free = [None, None]
        scaled, rowT_done, hTp_done = {}, {}, {}

        def scale_rows(nb):
            g0 = nb * GB
            scaled[nb] = dve.do(lambda e: e.tensor_tensor(
                sums_g[:, g0:g0 + GB, 0:D], sums_g[:, g0:g0 + GB, 0:D],
                inv[:, g0:g0 + GB].unsqueeze(2).broadcast_to([P, GB, D]), ALU.mult), done)

        def turn_rows(nb):
            s, g0 = nb % 2, nb * GB
            for h in range(2):
                pe.wait(scaled[nb], bank_free[h])
                for q in range(4):
                    m = pe.do(lambda e, h=h, q=q: e.transpose(bank[h][:, q * P:q * P + P],
                                                              sums_g[:, g0 + 4 * h + q, 0:D], ident[:, :]))
                v = bank[h][:, :].rearrange("p (n r) -> p n r", r=REL)
                hi, lo = (rowT[:, s, q, 0:REL, h * 4 * GN:(h + 1) * 4 * GN].rearrange("p r n -> p n r") for q in range(2))
                a = act.do(lambda e, v=v, hi=hi: e.activation(hi, v, ACT.Copy), m, rowT_free[s])
                bank_free[h] = dve.do(lambda e, v=v, hi=hi, lo=lo: e.tensor_tensor(lo, v, hi, ALU.subtract), a)
            zeroed.append(pool.do(lambda e: e.memset(sums_g[:, g0:g0 + GB, :], 0.0), m, done))
            m = pe.do(lambda e: e.transpose(bank[2][:, 0:P], xres[:, nb, :], ident[:, :]), bank_free[2], *x_ready)
            a = act.do(lambda e: e.activation(rowT[:, s, 0, REL, :], bank[2][:, 0:P], ACT.Copy, scale=FX), m, rowT_free[s])
            bank_free[2] = dve.do(lambda e: e.scalar_tensor_tensor(
                out=rowT[:, s, 1, REL, :], in0=bank[2][:, 0:P], scalar=FX, in1=rowT[:, s, 0, REL, :], op0=ALU.mult,
                op1=ALU.subtract), a)
            rowT_done[nb] = [bank_free[0], bank_free[1], bank_free[2]]

        def hidden(nb):
            s = nb % 2
            pe.wait(*rowT_done[nb], bank_free[3])
            for o in range(HB):
                for i, (wq, zq) in enumerate(PRODUCTS):
                    for r in range(RR):
                        f = lambda e, o=o, i=i, wq=wq, zq=zq, r=r: e.matmul(
                            bank[3][:, o * P:o * P + P], w1p[:, wq, r, o * P:o * P + P], rowT[:, s, zq, r, :],
                            start=(i == 0 and r == 0), stop=(i == 2 and r == RR - 1), skip_group_check=True)
                        if i == 2 and r == RR - 1:
                            m = pe.do(f)
                        else:
                            pe.quiet(f)
            rowT_free[s] = m
            for o in range(HB):
                a = bank_free[3] = act.do(lambda e, o=o: e.activation(
                    h32[:, o, :], bank[3][:, o * P:o * P + P], ACT.Relu, bias=unscale[:, 4 + o:5 + o],
                    scale=unscale[:, 0:1]), m, hTp_done[nb - 1][1] if nb else None)
            a = act.do(lambda e: e.activation(hTp[:, s, 0, :, :], h32[:, :, :], ACT.Copy), a, hTp_free[s])
            hTp_done[nb] = [a, dve.do(lambda e: e.tensor_tensor(hTp[:, s, 1, :, :], h32[:, :, :], hTp[:, s, 0, :, :],
                                                               ALU.subtract), a)]

        def table_rows(nb):
            s = nb % 2
            m = None
            for y in range(2):
                pe.wait(*hTp_done[nb], bank_free[4 + y])
                for i, (hq, wq) in enumerate(PRODUCTS):
                    for k in range(HB):
                        m = pe.do(lambda e, y=y, k=k, i=i, hq=hq, wq=wq: e.matmul(
                            bank[4 + y][:, :], hTp[:, s, hq, k, :],
                            w2p[:, wq, k, 4 * y:4 * y + 4, :].rearrange("p r d -> p (r d)"),
                            start=(i == 0 and k == 0), stop=(i == 2 and k == HB - 1)))
                rows2 = parts[:, s, 8 * y:8 * y + 8, :].rearrange("p (r q) d -> p r q d", q=2)
                bank_free[4 + y] = two_parts(rows2[:, :, 0, :], rows2[:, :, 1, :],
                                             bank[4 + y].rearrange("p (r d) -> p r d", d=D), unscale[:, 2:3],
                                             [m, part_free[s]])
            pe.wait(bank_free[6])
            for i, (hq, wq) in enumerate(PRODUCTS):
                for k in range(HB):
                    m = pe.do(lambda e, k=k, i=i, hq=hq, wq=wq: e.matmul(
                        bank[6][:, 0:P], hTp[:, s, hq, k, :], w2p[:, wq, k, REL, :], start=(i == 0 and k == 0),
                        stop=(i == 2 and k == HB - 1)))
            hTp_free[s] = m
            bank_free[6] = dve.do(lambda e: e.scalar_tensor_tensor(
                out=root_out[:, nb, :], in0=bank[6][:, 0:P], scalar=unscale[:, 1:2], in1=ROW["L3_gnn_b2"],
                op0=ALU.mult, op1=ALU.add), m, *x_ready)
            part_free[s] = sp.dma(table2[nb * P * REL:(nb + 1) * P * REL, :].rearrange("(p r) f -> p (r f)", r=REL),
                                  parts[:, s, :, :].rearrange("p r d -> p (r d)"), ch_t2[s], bank_free[4], bank_free[5])

        zeroed = []
        for nb in range(3):
            scale_rows(nb)
        turn_rows(0)
        turn_rows(1)
        hidden(0)
        for nb in range(NB):
            if nb + 1 < NB:
                hidden(nb + 1)
            if nb + 2 < NB:
                turn_rows(nb + 2)
            if nb + 3 < NB:
                scale_rows(nb + 3)
            table_rows(nb)
        zero_tok = zeroed[-1]
        xr = dve.do(lambda e: e.tensor_tensor(root_out, root_out, xres[:, :, :], ALU.add), dve.last())
        t_table2 = part_free[(NB - 1) % 2]

        sums_zero = [zero_tok]
        done = relation_sums(table2, 1, scales[:, 1, 3:4], [t_table2, part_free[0], part_free[1]])
        bf = [None] * 4
        scaled = {}
        scale_rows(0)
        scale_rows(1)
        for nb in range(NB):
            if nb + 2 < NB:
                scale_rows(nb + 2)
            g0, c = nb * GB, nb % 4
            pe.wait(scaled[nb], bf[c], t_place)
            for q in range(GB):
                f = lambda e, q=q, g0=g0, c=c: e.matmul(bank[2 * c][:, 0:D], place[:, q, :], sums_g[:, g0 + q, 0:D],
                                                        start=(q == 0), stop=(q == GB - 1))
                if q < GB - 1:
                    pe.quiet(f)
                else:
                    m = pe.do(f)
            bf[c] = dve.do(lambda e, nb=nb, c=c: e.tensor_tensor(root_out[:, nb, :], root_out[:, nb, :],
                                                                 bank[2 * c][:, 0:D], ALU.add), m, xr)
            if nb:
                t = stats_of(znode, [nb - 1], {nb - 1: bf[(nb - 1) % 4]})
        t = norm_params(stats_of(znode, [NB - 1], {NB - 1: bf[(NB - 1) % 4]}))
        ch_o = channel("ch_out")
        for quad in quads[:-1]:
            q0, q1 = quad[0], quad[-1] + 1
            sp.dma(out[q0 * P:q1 * P, :].rearrange("(b p) d -> p b d", p=P), xres[:, q0:q1, :], ch_o,
                   *normalize(xres, znode, quad, t))
        q0 = quads[-1][0]
        last = normalize(xres, znode, quads[-1], t)
        if q0 < FULL:
            sp.dma(out[q0 * P:FULL * P, :].rearrange("(b p) d -> p b d", p=P), xres[:, q0:FULL, :], ch_o, *last)
        t_out = sp.dma(out[FULL * P:N, :], xres[0:TAILN, FULL, :], ch_o, *last)
        sp.wait(t_out)
        rel.close()
        adj_ctx.close()

        block = ctx.enter_context(nc.Block())

        @block.tensor
        def _(e):
            pe.replay(e)

        @block.vector
        def _(e):
            dve.replay(e)

        @block.scalar
        def _(e):
            act.replay(e)

        @block.gpsimd
        def _(e):
            pool.replay(e)

        @block.sync
        def _(e):
            sp.replay(e)


_INS = ['x', 'src', 'dst', 'edge_type_8'] + [f"L0_gnn_{p}{i}" for i in (1, 2, 3) for p in ("W", "b", "g", "beta")] + \
    ['L1_gnn_W', 'L1_gnn_b', 'L2_gnn_eps', 'L2_gnn_W1', 'L2_gnn_b1', 'L2_gnn_g1', 'L2_gnn_beta1', 'L2_gnn_W2',
     'L2_gnn_b2', 'L2_gnn_g2', 'L2_gnn_beta2', 'L3_gnn_W1', 'L3_gnn_root1', 'L3_gnn_b1', 'L3_gnn_W2',
     'L3_gnn_root2', 'L3_gnn_b2']


def kernel(**inputs):
    import numpy as _np
    import concourse.bacc as _bacc
    from concourse import mybir as _mybir
    from concourse.bass_utils import run_bass_kernel_spmd as _run

    nc = _bacc.Bacc("TRN2", target_bir_lowering=False, num_devices=1)
    arrays, io = {}, {}
    for name in _INS:
        a = _np.ascontiguousarray(inputs[name])
        arrays[f"in_{name}_dram"] = a
        io[name] = nc.dram_tensor(f"in_{name}_dram", a.shape, _mybir.dt.from_np(a.dtype), kind="ExternalInput").ap()
    x = arrays["in_x_dram"]
    out = nc.dram_tensor("out_0_dram", x.shape, _mybir.dt.from_np(x.dtype), kind="ExternalOutput").ap()
    gnn_stack(nc, io, out)
    r = _run(nc, [arrays], core_ids=[0])
    return r.results[0]["out_0_dram"]
```
